# Optimizing a Trainium2 kernel written in Bass

```python
import numpy as np
import jax
import jax.numpy as jnp

def _softmax(x, axis=-1):
    return jax.nn.softmax(x, axis=axis)

def _gelu(x):
    return jax.nn.gelu(x, approximate=True)

def _silu(x):
    return jax.nn.silu(x)

def _sigmoid(x):
    return jax.nn.sigmoid(x)

def _layernorm(x, axis=-1, eps=1e-05):
    m = jnp.mean(x, axis=axis, keepdims=True)
    v = jnp.var(x, axis=axis, keepdims=True)
    return (x - m) / jnp.sqrt(v + eps)

def _scatter_add(tgt, idx, src, axis=0):
    return tgt.at[idx].add(src)

def _segment_sum(src, seg, n):
    return jax.ops.segment_sum(src, seg, n)
kernel_name = 'mk_flamingo_gated_d1_seqx_r8_b2fb42'

def setup_inputs(seed: int=0):
    np.random.seed(seed)
    _w = jnp.asarray

    def _rec_inputs():
        import jax
        import jax.numpy as jnp
        _rk = jax.random.key(seed)
        x = 0.0002417 + 0.9998 * jax.random.normal(jax.random.fold_in(_rk, 1), (16, 128, 128), jnp.float32)
        _lenS = 128 - jax.random.randint(jax.random.fold_in(_rk, 7), (16,), 0, max(1, 128 // 4) + 1, jnp.int32)
        _lenS2 = 77 - jax.random.randint(jax.random.fold_in(_rk, 8), (16,), 0, max(1, 77 // 4) + 1, jnp.int32)
        _ctx_1024P = jax.random.normal(jax.random.fold_in(_rk, 11), (16, 16, 128), jnp.float32)
        _ctx_1024c = jax.random.dirichlet(jax.random.fold_in(_rk, 511), 0.3 * jnp.ones((16,), jnp.float32), (16, 77))
        _ctx_1024t = jnp.einsum('bsk,bkd->bsd', _ctx_1024c, _ctx_1024P)
        _ctx_1024t = _ctx_1024t * jax.lax.rsqrt(jnp.mean(jnp.square(_ctx_1024t)) + 1e-12) * 0.953939
        ctx_1024 = 7.22013e-05 + 1.00017 * (_ctx_1024t + 0.3 * jax.random.normal(jax.random.fold_in(_rk, 611), (16, 77, 128), jnp.float32))
        _g = jax.random.normal(jax.random.fold_in(_rk, 9001), (2, 1), jnp.float32)
        _g = jnp.sign(_g) * jnp.maximum(jnp.abs(_g), 1.0) + (_g == 0) * 1.0
        g_xattn = _g[0]
        g_ffn = _g[1]
        return (x, ctx_1024, g_xattn, g_ffn)
    x, ctx_1024, g_xattn, g_ffn = _rec_inputs()

    def _L0_xattn_setup():
        import jax, jax.numpy as jnp
        import numpy as np
        HEADS = 16
        D_MODEL = 128
        HEAD_DIM = D_MODEL // HEADS
        key = jax.random.key(seed)
        ks = jax.random.split(key, 11)
        B, S = (4, 256)
        scale_in = 1.0 / np.sqrt(HEAD_DIM)
        scale_out = 1.0 / np.sqrt(D_MODEL)
        return {'values': jax.random.normal(ks[0], (B, S, D_MODEL), dtype=jnp.float32), 'keys': jax.random.normal(ks[1], (B, S, D_MODEL), dtype=jnp.float32), 'query': jax.random.normal(ks[2], (B, S, D_MODEL), dtype=jnp.float32), 'wq': jax.random.normal(ks[3], (HEAD_DIM, HEAD_DIM), dtype=jnp.float32) * scale_in, 'bq': jax.random.normal(ks[4], (HEAD_DIM,), dtype=jnp.float32) * 0.01, 'wk': jax.random.normal(ks[5], (HEAD_DIM, HEAD_DIM), dtype=jnp.float32) * scale_in, 'bk': jax.random.normal(ks[6], (HEAD_DIM,), dtype=jnp.float32) * 0.01, 'wv': jax.random.normal(ks[7], (HEAD_DIM, HEAD_DIM), dtype=jnp.float32) * scale_in, 'bv': jax.random.normal(ks[8], (HEAD_DIM,), dtype=jnp.float32) * 0.01, 'wo': jax.random.normal(ks[9], (D_MODEL, D_MODEL), dtype=jnp.float32) * scale_out, 'bo': jax.random.normal(ks[10], (D_MODEL,), dtype=jnp.float32) * 0.01}
    _L0_xattn_all = _L0_xattn_setup()
    _L0_xattn_in = {k: v for k, v in _L0_xattn_all.items() if k in ('wq', 'bq', 'wk', 'bk', 'wv', 'bv', 'wo', 'bo')}
    del _L0_xattn_all

    def _L0_ffn_setup():
        import jax, jax.numpy as jnp
        import numpy as np
        B, S, D = (4, 256, 128)
        E, F = (8, 512)
        key = jax.random.key(seed)
        ks = jax.random.split(key, 5)
        x = jax.random.normal(ks[0], (B, S, D), dtype=jnp.float32)
        switch_w = jax.random.normal(ks[1], (D, E), dtype=jnp.float32) * D ** (-0.5)
        switch_b = jnp.zeros((E,), dtype=jnp.float32)
        w1 = jax.random.normal(ks[2], (E, D, F), dtype=jnp.float32) * D ** (-0.5)
        b1 = jnp.zeros((E, F), dtype=jnp.float32)
        w2 = jax.random.normal(ks[3], (E, F, D), dtype=jnp.float32) * F ** (-0.5)
        b2 = jnp.zeros((E, D), dtype=jnp.float32)
        return {'x': x, 'switch_w': switch_w, 'switch_b': switch_b, 'w1': w1, 'b1': b1, 'w2': w2, 'b2': b2}
    _L0_ffn_all = _L0_ffn_setup()
    _L0_ffn_in = {k: v for k, v in _L0_ffn_all.items() if k in ('switch_w', 'switch_b', 'w1', 'b1', 'w2', 'b2')}
    del _L0_ffn_all
    return {'x': x, 'ctx_1024': ctx_1024, 'g_xattn': g_xattn, 'g_ffn': g_ffn, 'L0_xattn_wq': _L0_xattn_in['wq'], 'L0_xattn_bq': _L0_xattn_in['bq'], 'L0_xattn_wk': _L0_xattn_in['wk'], 'L0_xattn_bk': _L0_xattn_in['bk'], 'L0_xattn_wv': _L0_xattn_in['wv'], 'L0_xattn_bv': _L0_xattn_in['bv'], 'L0_xattn_wo': _L0_xattn_in['wo'], 'L0_xattn_bo': _L0_xattn_in['bo'], 'L0_ffn_switch_w': _L0_ffn_in['switch_w'], 'L0_ffn_switch_b': _L0_ffn_in['switch_b'], 'L0_ffn_w1': _L0_ffn_in['w1'], 'L0_ffn_b1': _L0_ffn_in['b1'], 'L0_ffn_w2': _L0_ffn_in['w2'], 'L0_ffn_b2': _L0_ffn_in['b2']}

def reference(x, ctx_1024, g_xattn, g_ffn, L0_xattn_wq, L0_xattn_bq, L0_xattn_wk, L0_xattn_bk, L0_xattn_wv, L0_xattn_bv, L0_xattn_wo, L0_xattn_bo, L0_ffn_switch_w, L0_ffn_switch_b, L0_ffn_w1, L0_ffn_b1, L0_ffn_w2, L0_ffn_b2):
    import jax
    import jax.numpy as jnp

    def _L0_xattn_ref(values, keys, query, wq, bq, wk, bk, wv, bv, wo, bo):
        import jax, jax.numpy as jnp
        import numpy as np
        HEADS = 16
        D_MODEL = 128
        HEAD_DIM = D_MODEL // HEADS
        B, Sq = (query.shape[0], query.shape[1])
        Sk, Sv = (keys.shape[1], values.shape[1])
        v = values.reshape(B, Sv, HEADS, HEAD_DIM) @ wv.T + bv
        k = keys.reshape(B, Sk, HEADS, HEAD_DIM) @ wk.T + bk
        q = query.reshape(B, Sq, HEADS, HEAD_DIM) @ wq.T + bq
        energy = jnp.einsum('nqhd,nkhd->nhqk', q, k)
        attn = jax.nn.softmax(energy / jnp.sqrt(jnp.float32(D_MODEL)), axis=-1)
        out = jnp.einsum('nhqk,nkhd->nqhd', attn, v).reshape(B, Sq, D_MODEL)
        return out @ wo.T + bo

    def _L0_ffn_ref(x, switch_w, switch_b, w1, b1, w2, b2):
        import jax, jax.numpy as jnp
        import numpy as np
        B, S, D = (4, 256, 128)
        E, F = (8, 512)
        b, s, d = x.shape
        t = x.reshape(-1, d)
        logits = t @ switch_w + switch_b
        route_prob = jax.nn.softmax(logits, axis=-1)
        route_prob_max = jnp.max(route_prob, axis=-1)
        routes = jnp.argmax(route_prob, axis=-1)
        out = jnp.zeros_like(t)
        n_experts = w1.shape[0]
        for e in range(n_experts):
            h = jax.nn.gelu(t @ w1[e] + b1[e])
            y = h @ w2[e] + b2[e]
            mask = (routes == e)[:, None]
            out = jnp.where(mask, y, out)
        out = out * route_prob_max[:, None]
        return out.reshape(b, s, d)
    x = x + jnp.tanh(g_xattn[0]) * _L0_xattn_ref(ctx_1024, ctx_1024, _layernorm(x, axis=-1), L0_xattn_wq, L0_xattn_bq, L0_xattn_wk, L0_xattn_bk, L0_xattn_wv, L0_xattn_bv, L0_xattn_wo, L0_xattn_bo)
    x = x + jnp.tanh(g_ffn[0]) * _L0_ffn_ref(_layernorm(x, axis=-1), L0_ffn_switch_w, L0_ffn_switch_b, L0_ffn_w1, L0_ffn_b1, L0_ffn_w2, L0_ffn_b2)
    return x

_drawn_inputs = setup_inputs


def setup_inputs(seed=0):
    import zlib

    import numpy as np

    out = dict(_drawn_inputs(seed))
    spreads = {'L0_ffn_switch_b': (0.0, 0.1), 'L0_ffn_b1': (0.0, 0.343), 'L0_ffn_b2': (0.0, 0.1)}
    factors = {'L0_xattn_bq': 35.563, 'L0_xattn_bk': 64.0, 'L0_xattn_bv': 3.021, 'L0_xattn_bo': 3.449}
    for name, (base, spread) in spreads.items():
        noise = np.random.default_rng([zlib.crc32(name.encode()), seed]).standard_normal(out[name].shape)
        drawn = base * np.exp(spread * noise) if base else spread * noise
        out[name] = jnp.asarray(drawn.astype(out[name].dtype))
    for name, factor in factors.items():
        out[name] = (out[name] * factor).astype(out[name].dtype)
    return out
```

```python
from contextlib import ExitStack

import concourse.bass as bass
from concourse import mybir

F32 = mybir.dt.float32
BF16 = mybir.dt.bfloat16
I32 = mybir.dt.int32
U32 = mybir.dt.uint32
ALU = mybir.AluOpType
ACT = mybir.ActivationFunctionType
AX = mybir.AxisListType.X

P = 128


def flamingo_layer(nc, x, ctx_in, g_xattn, g_ffn, wq_t, bq, wk_t, bk, wv_t, bv, wo_t, bo,
                   switch_w, switch_b, w1, b1_t, w2, b2, out, table):
    B, S, D = x.shape
    L = ctx_in.shape[1]
    HD = wq_t.shape[0]
    H = D // HD
    E, _, F = w1.shape
    FC = F // P
    assert S == P and D == P and B % 4 == 0
    J = 4
    G = B // J
    NTOK = B * S
    TILES = NTOK // P + E - 1
    RING = 4
    PEEL = 7
    assert (TILES - PEEL) % RING == 0
    HL = H * L
    CH = -(-HL // P)
    FLAT = CH * P
    HV = HD + 1
    SCALE = float(D) ** -0.5
    EPS = 1e-5
    ROW = 2 * D + 1
    PER_BANK = 512 // L
    E_HEADS = [(h, min(h + PER_BANK, H)) for h in range(0, H, PER_BANK)]
    E_BANKS = len(E_HEADS)
    T_CHUNKS = [(c, min(c + 4, CH)) for c in range(0, CH, 4)]
    T_BANKS = len(T_CHUNKS)
    assert E_BANKS + T_BANKS == 6
    HALF = B // 2

    PIECES = []
    for h in range(H):
        f = h * L
        while f < (h + 1) * L:
            n = min((h + 1) * L - f, P - f % P)
            PIECES.append((h, f - h * L, f // P, f % P, n))
            f += n

    with ExitStack() as ctx:
        def sb(name, shape, dt=F32):
            return ctx.enter_context(nc.sbuf_tensor(name, shape, dt))

        def sem(name):
            return ctx.enter_context(nc.semaphore(name))

        ident = sb("ident", [P, P])
        identb = sb("identb", [P, P], BF16)
        rep = sb("rep", [HD, P])
        headmask = sb("headmask", [P, H])
        headsel = sb("headsel", [P, FLAT], BF16)
        before = sb("before", [P, P], BF16)
        ones = sb("ones", [P, P], BF16)
        iota_row = sb("iota_row", [P, P])
        iota_part = sb("iota_part", [P, 1])
        tile_start = sb("tile_start", [P, TILES])
        rank_step = sb("rank_step", [P, B])
        prefer_low = sb("prefer_low", [P, E])
        seq_code = sb("seq_code", [P, B])
        e_before = sb("e_before", [P, E, E])
        gates = sb("gates", [P, 2])
        tanhs = sb("tanhs", [P, 2])
        w_small = sb("w_small", [HD, 3, HV])
        wrep = sb("wrep", [P, 3, HV])
        wbd = sb("wbd", [P, 3, H, HD])
        bv_cols = sb("bv_cols", [P, P])
        wo_sb = sb("wo_sb", [P, D])
        wo_g = sb("wo_g", [P, D])
        bo_bc = sb("bo_bc", [P, D])
        out_bias = sb("out_bias", [P, D])
        sw_sb = sb("sw_sb", [P, E])
        sbias = sb("sbias", [P, E])
        w2_sb = sb("w2_sb", [P, E, FC, D])
        b1_sb = sb("b1_sb", [P, E, FC])
        b2_bc = sb("b2_bc", [P, E, D])
        ctx_sb = sb("ctx_sb", [L, B, D])
        ctx_t = sb("ctx_t", [P, B, L])
        k_t = sb("k_t", [P, B, L])
        v_src = sb("v_src", [L, H, B, HV])
        x_sb = sb("x_sb", [P, B, D])
        stats1 = sb("stats1", [P, B, 6])
        mv1 = sb("mv1", [P, B, 2])
        rstd1 = sb("rstd1", [P, B])
        half_var1, newton1 = sb("half_var1", [P, J]), sb("newton1", [P, J])
        half_var2, newton2 = sb("half_var2", [P, 1]), sb("newton2", [P, 1])
        xn1 = sb("xn1", [P, 2, J, D])
        xn1_t = sb("xn1_t", [P, 2, J, P])
        q_t = sb("q_t", [P, B, P])
        q_tb = sb("q_tb", [P, B, P], BF16)
        v_bd = sb("v_bd", [P, CH, H, B, HV])
        k_bd = sb("k_bd", [P, 2, FLAT])
        k_bdb = sb("k_bdb", [P, 2, HL], BF16)
        emax = sb("emax", [P, 2, H])
        shift = sb("shift", [P, 2, P], BF16)
        shift_t = sb("shift_t", [P, P], BF16)
        probs = sb("probs", [P, FLAT])
        headsel2 = probs[:, :].bitcast(BF16)[:, 0:FLAT]
        rden = sb("rden", [P, H])
        attn = sb("attn", [P, D])
        attn_t = sb("attn_t", [P, P])
        stats2 = sb("stats2", [P, 6])
        mv2 = sb("mv2", [P, 2])
        rstd2 = sb("rstd2", [P, 1])
        rows = sb("rows", [P, 2, 2 * D])
        xn2_t = sb("xn2_t", [P, P])
        logits = sb("logits", [P, B, E])
        lmax = sb("lmax", [P, B])
        lsub = sb("lsub", [P, B, E])
        lexp = sb("lexp", [P, B, E])
        lsum = sb("lsum", [P, B])
        scale_tok = sb("scale_tok", [P, B])
        is_max = sb("is_max", [P, B, E])
        pick = sb("pick", [P, B])
        onehot = sb("onehot", [P, B, E])
        onehotb = sb("onehotb", [P, B, E], BF16)
        over = sb("over", [P, E, B])
        n_tiles = sb("n_tiles", [P, E])
        base_prod = sb("base_prod", [P, E, E])
        base = sb("base", [P, E])
        end = sb("end", [P, E])
        slot_e = sb("slot_e", [P, B, E])
        slot_m = sb("slot_m", [P, B, E])
        slot = sb("slot", [P, B])
        slot_int = sb("slot_int", [P, B], I32)
        slot_low = sb("slot_low", [P, B], I32)
        slot_row = sb("slot_row", [P, B])
        slot_start = sb("slot_start", [P, B])
        free = [v_bd[:, c, :, :, :].rearrange("p h b d -> p (h b d)") for c in range(6)]
        row_hot = free[0].bitcast(BF16)[:, 0:B * P].rearrange("p (b s) -> p b s", b=B)
        tile_hot = free[1][:, 0:B * TILES].rearrange("p (b t) -> p b t", b=B)
        tile_val = free[2].bitcast(BF16)[:, 0:B * 2 * TILES].rearrange("p (b s t) -> p b s t", b=B, s=2)
        past = free[3][:, 0:TILES * E].rearrange("p (t e) -> p t e", t=TILES)
        expert_f = sb("expert_f", [P, TILES])
        expert = sb("expert", [P, TILES], I32)
        tok_a = sb("tok_a", [P, TILES])
        tok = sb("tok", [P, TILES], U32)
        w1_ring = free[4][:, 0:RING * F].rearrange("p (r f) -> p r f", r=RING)
        hid = free[5][:, 0:2 * FC * P].rearrange("p (r c t) -> p r c t", r=2, c=FC)
        spare = [t[:, :, :, :].rearrange("p r j s -> p (r j s)") for t in (xn1, xn1_t)]
        gat = [spare[i // 2][:, (i % 2) * ROW:(i % 2 + 1) * ROW] for i in range(RING)]
        tok_col = [sb(f"tok_col{i}", [P, 1], U32) for i in range(RING)]
        xg_t = sb("xg_t", [P, 2, P])
        yb = sb("yb", [P, 2, D])
        res = [spare[i][:, 2 * ROW:2 * ROW + D] for i in range(2)]

        pe_bank = [ctx.enter_context(nc.psum_tensor(f"ps{i}", [P, 512], F32)) for i in range(2)]
        ps_e = ctx.enter_context(nc.psum_tensor("ps_e", [P, E_BANKS, 512], F32))
        ps_t = ctx.enter_context(nc.psum_tensor("ps_t", [P, T_BANKS, 512], F32))
        bank = [ps_e[:, i, :] for i in range(E_BANKS)] + [ps_t[:, i, :] for i in range(T_BANKS)] \
            + [pe_bank[0][:, :], pe_bank[1][:, :]]
        M0, M1 = bank[6], bank[7]

        ld_small, ld_ctx, ld_x, ld_misc = sem("ld_small"), [sem(f"ld_ctx{g}") for g in range(G)], \
            [sem(f"ld_x{g}") for g in range(G)], sem("ld_misc")
        ld_router, ld_w2, ld_b1, ld_b2 = sem("ld_router"), sem("ld_w2"), sem("ld_b1"), sem("ld_b2")
        passed = sem("passed")
        zeroed = sem("zeroed")
        const_done = sem("const_done")
        mask_step = sem("mask_step")
        vbd_zero = sem("vbd_zero")
        vsrc_ones = sem("vsrc_ones")
        pad_zero = sem("pad_zero")
        wrep_mm = sem("wrep_mm")
        wrep_done = sem("wrep_done")
        wbd_done = sem("wbd_done")
        tanh_done = sem("tanh_done")
        wog_done = sem("wog_done")
        bvc_done = sem("bvc_done")
        obias_mm = sem("obias_mm")
        obias_done = sem("obias_done")
        xres_done = sem("xres_done")
        ctxt_mm, ctxt_done = sem("ctxt_mm"), sem("ctxt_done")
        k_mm, k_done = sem("k_mm"), sem("k_done")
        v_mm, v_done = sem("v_mm"), sem("v_done")
        st1_done, mv1_done, rstd1_step, xn1_done = sem("st1_done"), sem("mv1_done"), sem("rstd1_step"), sem("xn1_done")
        xt_mm, xt_done = sem("xt_mm"), sem("xt_done")
        q_mm, q_done, qb_done = sem("q_mm"), sem("q_done"), sem("qb_done")
        ld_vbd = [sem("ld_vbd0"), sem("ld_vbd1")]
        kbd_ready, kbdb_ready = sem("kbd_ready"), sem("kbdb_ready")
        energy_mm, emax_done, shift1_done, shift_done = sem("energy_mm"), sem("emax_done"), sem("shift1_done"), sem("shift_done")
        shiftt_mm, shiftt_done = sem("shiftt_mm"), sem("shiftt_done")
        score_mm, exp_done = sem("score_mm"), sem("exp_done")
        pv_mm, rden_done, attn_done = sem("pv_mm"), sem("rden_done"), sem("attn_done")
        at_mm, at_done = sem("at_mm"), sem("at_done")
        wo_mm, x1_done, st2_done, mv2_done, rstd2_step, xn2_done = (
            sem("wo_mm"), sem("x1_done"), sem("st2_done"), sem("mv2_done"), sem("rstd2_step"), sem("xn2_done"))
        x2t_mm, x2t_done, lg_mm, lg_done = sem("x2t_mm"), sem("x2t_done"), sem("lg_mm"), sem("lg_done")
        row_store = [sem("row_store0"), sem("row_store1")]
        cs = sem("route_step")
        lsub_done, lexp_done, scale_done, scale_store = sem("lsub_done"), sem("lexp_done"), sem("scale_done"), sem("scale_store")
        oh_done, rank_mm, rowhot_done, tileval_done, tok_mm = (
            sem("oh_done"), sem("rank_mm"), sem("rowhot_done"), sem("tileval_done"), sem("tok_mm"))
        tok_done, expert_done = sem("tok_done"), sem("expert_done")
        gat_zero = sem("gat_zero")
        tokcol_done = sem("tokcol_done")
        gathered = [sem(f"gathered{i}") for i in range(RING)]
        w1_ready = [sem(f"w1_ready{i}") for i in range(RING)]
        xgt_mm, xgt_done = sem("xgt_mm"), sem("xgt_done")
        up_mm, hid_done, down_mm = sem("up_mm"), sem("hid_done"), sem("down_mm")
        yb_done, res_done = sem("yb_done"), sem("res_done")
        scattered = [sem("scattered0"), sem("scattered1")]

        block = ctx.enter_context(nc.Block())

        def for_tiles(eng, tile_step):
            for t in range(PEEL):
                tile_step(t, t)
            with eng.Fori(0, (TILES - PEEL) // RING) as i:
                for k in range(RING):
                    tile_step(i * RING + (PEEL + k), PEEL + k)

        def for_seqs(eng, seq_step):
            for b in range(3):
                seq_step(b, b)
            with eng.Fori(0, (B - 6) // 2) as i:
                seq_step(i * 2 + 3, 3)
                seq_step(i * 2 + 4, 4)
            for b in range(B - 3, B):
                seq_step(b, b)

        def detach(eng):
            eng.sem_inc(passed, 1)

        def build_keys(pool, b, k):
            src = k_t[:, bass.ds(b, 1), :].broadcast_to([P, H, L])
            mask = headmask[:, :].rearrange("p (h a) -> p h a", a=1).broadcast_to([P, H, L])
            nc.gpsimd.tensor_tensor(k_bd[:, k % 2, 0:HL].rearrange("p (h l) -> p h l", h=H), src, mask,
                                    ALU.mult).then_inc(kbd_ready, 1)
            nc.gpsimd.tensor_tensor(k_bdb[:, k % 2, :].rearrange("p (h l) -> p h l", h=H), src, mask,
                                    ALU.mult).then_inc(kbdb_ready, 1)

        def gather_count(t, k):
            if isinstance(t, int):
                return 16 * (t // RING + 1)
            return (t - (k % RING)) * (16 // RING) + 16

        @block.sync
        def _(sp):
            for n, w in enumerate((wk_t, wv_t, wq_t)):
                sp.dma_start(w_small[:, n, 0:HD], w).then_inc(ld_small, 16)
            for n, b in enumerate((bk, bv, bq)):
                sp.dma_start(w_small[:, n, HD:HV], b.rearrange("(p a) -> p a", a=1)).then_inc(ld_small, 16)
            for g in range(G):
                js = slice(g * J, g * J + J)
                sp.dma_start(ctx_sb[:, js, :], ctx_in[js].rearrange("b l d -> l b d")).then_inc(ld_ctx[g], 16)
                sp.dma_start(x_sb[:, js, :], x[js].rearrange("b s d -> s b d")).then_inc(ld_x[g], 16)
            for half in range(2):
                sp.wait_ge(v_done, G // 2 * (half + 1))
                sp.wait_ge(vsrc_ones, 1)
                sp.wait_ge(vbd_zero, 2)
                bs = slice(half * HALF, (half + 1) * HALF)
                for h, k0, c, r, n in PIECES:
                    sp.dma_start(v_bd[r:r + n, c, h, bs, :], v_src[k0:k0 + n, h, bs, :]).then_inc(ld_vbd[half], 16)
            sp.dma_start(w2_sb[:, :, :, :], w2.rearrange("e (c p) d -> p e c d", p=P)).then_inc(ld_w2, 16)
            sp.dma_start(b1_sb[:, :, :], b1_t.rearrange("p (e c) -> p e c", e=E)).then_inc(ld_b1, 16)
            sp.dma_start(b2_bc[:, :, :].rearrange("p e d -> p (e d)"),
                         b2.rearrange("(a e) d -> a (e d)", a=1).partition_broadcast(P)
                         if False else b2.rearrange("(a e) d -> a (e d)", a=1).broadcast_to([P, E * D])
                         ).then_inc(ld_b2, 16)

            def store_rows(b, k):
                sp.wait_ge(xn2_done, b + 1)
                sp.dma_start(table[bass.ds(b * P, P), 0:2 * D], rows[:, k % 2, :]).then_inc(row_store[k % 2], 16)

            for_seqs(sp, store_rows)
            sp.wait_ge(scale_done, 1)
            sp.dma_start(table.rearrange("(b p) r -> p b r", p=P)[:, :, 2 * D:ROW],
                         scale_tok[:, :].rearrange("p (b a) -> p b a", a=1), allow_slow_non_contiguous=True).then_inc(scale_store, 16)

            sp.wait_ge(expert_done, 1)

            def load_w1(t, k):
                if k >= RING:
                    sp.wait_ge(up_mm, t - RING + 1)
                e = sp.value_load(expert[0:1, bass.ds(t, 1)], min_val=0, max_val=E - 1)
                sp.dma_start(w1_ring[:, k % RING, :], w1[bass.ds(e, 1)].rearrange("e p f -> p (e f)")
                             ).then_inc(w1_ready[k % RING], 16)

            for_tiles(sp, load_w1)

        @block.gpsimd
        def _(pool):
            pool.memset(ident[:, :], 0.0).then_inc(zeroed, 1)
            pool.memset(rep[:, :], 0.0).then_inc(zeroed, 1)
            pool.memset(headmask[:, :], 1.0).then_inc(zeroed, 1)
            pool.wait_ge(zeroed, 3)
            pool.affine_select(ident[:, :], ident[:, :], pattern=[[-1, P]], compare_op=ALU.not_equal,
                               fill=1.0, base=0, channel_multiplier=1).then_inc(const_done, 1)
            pool.affine_select(rep[:, :].rearrange("i (h j) -> i h j", h=H), rep[:, :].rearrange("i (h j) -> i h j", h=H),
                               pattern=[[0, H], [-1, HD]], compare_op=ALU.not_equal,
                               fill=1.0, base=0, channel_multiplier=1).then_inc(const_done, 1)
            pool.affine_select(headmask[:, :], headmask[:, :], pattern=[[-HD, H]], compare_op=ALU.is_ge,
                               fill=0.0, base=0, channel_multiplier=1).then_inc(mask_step, 1)
            pool.wait_ge(mask_step, 1)
            pool.affine_select(headmask[:, :], headmask[:, :], pattern=[[HD, H]], compare_op=ALU.is_ge,
                               fill=0.0, base=HD - 1, channel_multiplier=-1).then_inc(const_done, 1)
            pool.memset(v_src[:, :, :, HD:HV], 1.0).then_inc(vsrc_ones, 1)
            pool.memset(v_bd[:, 0:CH // 2, :, :, :], 0.0).then_inc(vbd_zero, 1)
            pool.memset(k_bd[:, :, HL:FLAT], 0.0).then_inc(pad_zero, 1)
            pool.memset(shift[:, :, :], 0.0).then_inc(pad_zero, 1)
            for n, hs in enumerate((headsel, headsel2)):
                pool.memset(hs[:, 0:HL], 1.0).then_inc(mask_step, 1)
                pool.memset(hs[:, HL:FLAT], 0.0).then_inc(mask_step, 1)
                pool.wait_ge(mask_step, 1 + 4 * n + 2)
                pool.affine_select(hs[:, 0:HL], hs[:, 0:HL], pattern=[[1, HL]], compare_op=ALU.is_ge, fill=0.0,
                                   base=n * H * L, channel_multiplier=-L).then_inc(mask_step, 1)
                pool.wait_ge(mask_step, 1 + 4 * n + 3)
                pool.affine_select(hs[:, 0:HL], hs[:, 0:HL], pattern=[[-1, HL]], compare_op=ALU.is_ge, fill=0.0,
                                   base=L - 1 - n * H * L, channel_multiplier=L).then_inc(mask_step, 1)
            pool.wait_ge(mask_step, 9)
            pool.tensor_tensor(headsel[:, :], headsel[:, :], headsel2[:, :], ALU.add).then_inc(const_done, 1)
            pool.wait_ge(obias_done, 1)
            for g in range(G):
                pool.wait_ge(st1_done, (g + 1) * J)
                pool.wait_ge(xn1_done, (g + 1) * J)
                js = slice(g * J, g * J + J)
                pool.tensor_tensor(x_sb[:, js, :], x_sb[:, js, :],
                                   out_bias[:, :].rearrange("p (a d) -> p a d", a=1).broadcast_to([P, J, D]),
                                   ALU.add).then_inc(xres_done, 1)
                if g == 0:
                    pool.wait_ge(k_done, 1)
                    for b in range(2):
                        build_keys(pool, b, b)
            pool.wait_ge(k_done, G)

            def keys_ahead(b, k):
                if k + 2 < B:
                    pool.wait_ge(score_mm, T_BANKS * b + T_BANKS)
                    build_keys(pool, b + 2, k + 2)

            for_seqs(pool, keys_ahead)

            pool.iota(iota_row[:, :], pattern=[[1, P]], base=0, channel_multiplier=0,
                      allow_small_or_imprecise_dtypes=True).then_inc(const_done, 1)
            pool.iota(iota_part[:, :], pattern=[[1, 1]], base=0, channel_multiplier=1,
                      allow_small_or_imprecise_dtypes=True).then_inc(const_done, 1)
            pool.iota(tile_start[:, :], pattern=[[P, TILES]], base=0, channel_multiplier=0,
                      allow_small_or_imprecise_dtypes=True).then_inc(const_done, 1)
            pool.iota(rank_step[:, :], pattern=[[P, B]], base=0, channel_multiplier=0,
                      allow_small_or_imprecise_dtypes=True).then_inc(const_done, 1)
            pool.iota(prefer_low[:, :], pattern=[[-1, E]], base=E, channel_multiplier=0,
                      allow_small_or_imprecise_dtypes=True).then_inc(const_done, 1)
            pool.iota(seq_code[:, :], pattern=[[-1, B]], base=B, channel_multiplier=0,
                      allow_small_or_imprecise_dtypes=True).then_inc(const_done, 1)
            pool.memset(ones[:, :], 1.0).then_inc(const_done, 1)
            pool.memset(before[:, :], 1.0).then_inc(zeroed, 1)
            pool.memset(e_before[:, :, :], 1.0).then_inc(zeroed, 1)
            pool.wait_ge(zeroed, 5)
            pool.affine_select(before[:, :], before[:, :], pattern=[[1, P]], compare_op=ALU.is_ge, fill=0.0,
                               base=-1, channel_multiplier=-1).then_inc(const_done, 1)
            pool.affine_select(e_before[:, :, :], e_before[:, :, :], pattern=[[1, E], [-1, E]], compare_op=ALU.is_ge,
                               fill=0.0, base=-1, channel_multiplier=0).then_inc(const_done, 1)
            for i in range(RING):
                pool.memset(gat[i][:, :], 0.0).then_inc(gat_zero, 1)
            pool.wait_ge(gat_zero, RING)
            pool.wait_ge(tok_done, 1)
            pool.wait_ge(scale_store, 16)
            for i in range(2):
                pool.wait_ge(row_store[i], 16 * (B // 2))

            def gather(t, k):
                if k >= RING:
                    pool.wait_ge(res_done, t - RING + 1)
                    pool.wait_ge(scattered[k % 2], (t - RING - k % 2) * 8 + 16)
                    detach(pool)
                pool.tensor_copy(tok_col[k % RING][:, :], tok[:, bass.ds(t, 1)]).then_inc(tokcol_done, 1)
                pool.wait_ge(tokcol_done, t + 1)
                detach(pool)
                pool.indirect_dma_start(
                    out=gat[k % RING], out_offset=None, in_=table[:, :],
                    in_offset=bass.IndirectOffsetOnAxis(ap=tok_col[k % RING][:, 0:1], axis=0),
                    bounds_check=NTOK - 1, oob_is_err=False).then_inc(gathered[k % RING], 16)

            def scatter(t, k):
                pool.wait_ge(res_done, t + 1)
                detach(pool)
                pool.indirect_dma_start(
                    out=out, out_offset=bass.IndirectOffsetOnAxis(ap=tok_col[k % RING][:, 0:1], axis=0),
                    in_=res[k % 2][:, :], in_offset=None,
                    bounds_check=NTOK - 1, oob_is_err=False).then_inc(scattered[k % 2], 16)

            for t in range(2):
                gather(t, t)
            for t in range(2, PEEL):
                gather(t, t)
                scatter(t - 2, t - 2)
            with pool.Fori(0, (TILES - PEEL) // RING) as i:
                for k in range(PEEL, PEEL + RING):
                    gather(i * RING + k, k)
                    scatter(i * RING + (k - 2), k - 2)
            for t in range(TILES - 2, TILES):
                scatter(t, t)
            pool.wait_ge(scattered[0], 16 * ((TILES + 1) // 2))
            pool.wait_ge(scattered[1], 16 * (TILES // 2))

        @block.scalar
        def _(act):
            act.dma_start(gates[:, 0:1], g_xattn.rearrange("(a b) -> a b", a=1).broadcast_to([P, 1])).then_inc(ld_misc, 16)
            act.dma_start(gates[:, 1:2], g_ffn.rearrange("(a b) -> a b", a=1).broadcast_to([P, 1])).then_inc(ld_misc, 16)
            act.dma_start(wo_sb[:, :], wo_t).then_inc(ld_misc, 16)
            act.dma_start(bo_bc[:, :], bo.rearrange("(a d) -> a d", a=1).broadcast_to([P, D])).then_inc(ld_misc, 16)
            act.dma_start(sw_sb[:, :], switch_w).then_inc(ld_router, 16)
            act.dma_start(sbias[:, :], switch_b.rearrange("(a d) -> a d", a=1).broadcast_to([P, E])).then_inc(ld_router, 16)
            act.wait_ge(ld_misc, 64)
            act.activation(tanhs[:, :], gates[:, :], ACT.Tanh).then_inc(tanh_done, 1)
            act.wait_ge(tanh_done, 1)
            act.activation(wo_g[:, :], wo_sb[:, :], ACT.Copy, scale=tanhs[:, 0:1]).then_inc(wog_done, 1)
            act.wait_ge(wrep_done, 1)
            for g in range(G):
                js = slice(g * J, g * J + J)
                act.wait_ge(k_mm, g + 1)
                act.activation(k_t[:, js, :], bank[2 + g % 2][:, 0:J * L].rearrange("p (j l) -> p j l", j=J),
                               ACT.Identity, bias=wrep[:, 0, HD:HV]).then_inc(k_done, 1)
                act.wait_ge(xt_mm, g + 1)
                if g >= 2:
                    act.wait_ge(q_mm, g - 1)
                act.activation(xn1_t[:, g % 2, :, :].rearrange("p j s -> p (j s)"), bank[6][:, :],
                               ACT.Copy).then_inc(xt_done, 1)
                act.wait_ge(q_mm, g + 1)
                act.activation(q_t[:, js, :].rearrange("p j s -> p (j s)"), bank[7][:, :],
                               ACT.Identity, bias=wrep[:, 2, HD:HV]).then_inc(q_done, 1)

            def attention(b, k):
                if k >= 1:
                    act.wait_ge(at_mm, b)
                    act.activation(attn_t[:, :], M0[:, 0:P], ACT.Copy).then_inc(at_done, 1)
                for n, (c0, c1) in enumerate(T_CHUNKS):
                    act.wait_ge(score_mm, b * T_BANKS + n + 1)
                    if n == 0 and k >= 1:
                        act.wait_ge(pv_mm, b)
                    act.activation(probs[:, c0 * P:c1 * P], bank[3 + n][:, 0:(c1 - c0) * P], ACT.Exp,
                                   scale=SCALE).then_inc(exp_done, 1)
                if k >= 1:
                    act.wait_ge(x2t_mm, b)
                    act.activation(xn2_t[:, :], M0[:, 0:P], ACT.Copy).then_inc(x2t_done, 1)

            for_seqs(act, attention)
            act.wait_ge(at_mm, B)
            act.activation(attn_t[:, :], M0[:, 0:P], ACT.Copy).then_inc(at_done, 1)
            act.wait_ge(x2t_mm, B)
            act.activation(xn2_t[:, :], M0[:, 0:P], ACT.Copy).then_inc(x2t_done, 1)
            act.wait_ge(lsub_done, 1)
            act.activation(lexp[:, :, :], lsub[:, :, :], ACT.Exp).then_inc(lexp_done, 1)
            act.wait_ge(ld_b1, 16)
            act.wait_ge(expert_done, 1)

            def gelu(t, k):
                e = act.value_load(expert[0:1, bass.ds(t, 1)], min_val=0, max_val=E - 1)
                if k >= 2:
                    act.wait_ge(down_mm, t - 1)
                for c in range(FC):
                    act.wait_ge(up_mm, t + 1) if c == 0 else None
                    last = act.activation(hid[:, k % 2, c, :], bank[2 + k % 2][:, c * P:c * P + P], ACT.Gelu_apprx_tanh,
                                          bias=b1_sb[:, bass.ds(e, 1), c])
                last.then_inc(hid_done, 1)

            for_tiles(act, gelu)

        @block.tensor
        def _(pe):
            pe.wait_ge(ld_small, 96)
            pe.wait_ge(const_done, 3)
            pe.matmul(bank[7][:, 0:3 * HV], rep[:, :], w_small[:, :, :].rearrange("p n d -> p (n d)"),
                      start=True, stop=True).then_inc(wrep_mm, 1)
            for g in range(G):
                js = slice(g * J, g * J + J)
                pe.wait_ge(ld_ctx[g], 16)
                if g >= 2:
                    pe.wait_ge(ctxt_done, g - 1)
                for j in range(J):
                    last = pe.transpose(bank[g % 2][:, j * L:j * L + L], ctx_sb[:, g * J + j, :], ident[0:L, 0:L])
                last.then_inc(ctxt_mm, 1)
                pe.wait_ge(xn1_done, (g + 1) * J)
                if g >= 1:
                    pe.wait_ge(xt_done, g)
                for j in range(J):
                    last = pe.transpose(bank[6][:, j * P:j * P + P], xn1[:, g % 2, j, :], ident[:, :])
                last.then_inc(xt_mm, 1)
                pe.wait_ge(ctxt_done, g + 1)
                pe.wait_ge(wbd_done, 1)
                if g >= 2:
                    pe.wait_ge(k_done, g - 1)
                pe.matmul(bank[2 + g % 2][:, 0:J * L], wbd[:, 0, :, :].rearrange("p h d -> p (h d)"),
                          ctx_t[:, js, :].rearrange("p j l -> p (j l)"), start=True, stop=True).then_inc(k_mm, 1)
                if g >= 2:
                    pe.wait_ge(v_done, g - 1)
                for j in range(J):
                    last = pe.matmul(bank[4 + g % 2][0:L, j * D:j * D + D], ctx_t[:, g * J + j, :],
                                     wbd[:, 1, :, :].rearrange("p h d -> p (h d)"), start=(j == 0), stop=(j == J - 1),
                                     skip_group_check=True)
                last.then_inc(v_mm, 1)
                pe.wait_ge(xt_done, g + 1)
                if g == 0:
                    pe.wait_ge(obias_free := wrep_done, 1)
                else:
                    pe.wait_ge(q_done, g)
                    pe.wait_ge(qb_done, g)
                pe.matmul(bank[7][:, :], wbd[:, 2, :, :].rearrange("p h d -> p (h d)"),
                          xn1_t[:, g % 2, :, :].rearrange("p j s -> p (j s)"), start=True, stop=True).then_inc(q_mm, 1)
                if g == 0:
                    pe.wait_ge(bvc_done, 1)
                    pe.wait_ge(wog_done, 1)
                    pe.matmul(bank[3][:, 0:D], bv_cols[:, :], wo_g[:, :], start=True, stop=True).then_inc(obias_mm, 1)
                if g == 0:
                    pe.wait_ge(obias_done, 1)

            def energies(b, k):
                pe.wait_ge(kbdb_ready, b + 1)
                for n, (h0, h1) in enumerate(E_HEADS):
                    last = pe.matmul(bank[n][:, 0:(h1 - h0) * L],
                                     q_tb[:, bass.ds(b, 1), :].rearrange("p a s -> p (a s)"),
                                     k_bdb[:, k % 2, h0 * L:h1 * L], start=True, stop=True)
                last.then_inc(energy_mm, 1)

            def scores(b, k, n):
                c0, c1 = T_CHUNKS[n]
                if k >= 1:
                    pe.wait_ge(exp_done, (b - 1) * T_BANKS + n + 1)
                for c in range(c0, c1):
                    pe.matmul(bank[3 + n][:, (c - c0) * P:(c - c0) * P + P], k_bd[:, k % 2, c * P:c * P + P],
                              q_t[:, bass.ds(b, 1), :].rearrange("p a s -> p (a s)"), start=(c == c0), stop=False,
                              skip_group_check=True)

            def shift_scores(n):
                c0, c1 = T_CHUNKS[n]
                for c in range(c0, c1):
                    last = pe.matmul(bank[3 + n][:, (c - c0) * P:(c - c0) * P + P], headsel[:, c * P:c * P + P],
                                     shift_t[:, :], start=False, stop=(c == c1 - 1), skip_group_check=True)
                last.then_inc(score_mm, 1)

            def attn_transpose(b):
                pe.wait_ge(attn_done, b + 1)
                if not (isinstance(b, int) and b == 0):
                    pe.wait_ge(lg_done, b)
                pe.transpose(M0[:, 0:P], attn[:, :], ident[:, :]).then_inc(at_mm, 1)

            def project_out(b):
                pe.wait_ge(at_done, b + 1)
                pe.matmul(M0[:, 0:D], attn_t[:, :], wo_g[:, :], start=True, stop=True).then_inc(wo_mm, 1)

            def norm_transpose(b, k):
                pe.wait_ge(xn2_done, b + 1)
                pe.transpose(M0[:, 0:P], rows[:, k % 2, D:2 * D], ident[:, :]).then_inc(x2t_mm, 1)

            def router(b):
                pe.wait_ge(x2t_done, b + 1)
                pe.matmul(M0[:, 0:E], xn2_t[:, :], sw_sb[:, :], start=True, stop=True).then_inc(lg_mm, 1)

            def weigh_values(b, k):
                for c in range(CH):
                    if c % 4 == 0:
                        pe.wait_ge(exp_done, b * T_BANKS + c // 4 + 1)
                    last = pe.matmul(M1[:, 0:H * HV], probs[:, c * P:c * P + P],
                                     v_bd[:, c, :, bass.ds(b, 1), :].rearrange("p h b d -> p h (b d)"),
                                     start=(c == 0), stop=(c == CH - 1))
                last.then_inc(pv_mm, 1)

            def attention(b, k):
                scores(b, k, 0)
                if k >= 1:
                    attn_transpose(b - 1)
                scores(b, k, 1)
                pe.wait_ge(shift_done, b + 1)
                if k >= 1:
                    pe.wait_ge(attn_done, b)
                pe.transpose(M1.bitcast(BF16)[:, 0:P], shift[:, k % 2, :], identb[:, :]).then_inc(shiftt_mm, 1)
                if k >= 1:
                    project_out(b - 1)
                scores(b, k, 2)
                pe.wait_ge(shiftt_done, b + 1)
                for n in range(T_BANKS):
                    shift_scores(n)
                if k + 1 < B:
                    energies(b + 1, k + 1)
                if k >= 1:
                    norm_transpose(b - 1, k - 1)
                if k == 0:
                    pe.wait_ge(ld_vbd[0], 16 * len(PIECES))
                    pe.wait_ge(ld_router, 32)
                if k == 3:
                    pe.wait_ge(ld_vbd[1], 16 * len(PIECES))
                weigh_values(b, k)
                if k >= 1:
                    router(b - 1)

            pe.wait_ge(ctxt_done, G)
            pe.wait_ge(k_done, G)
            pe.wait_ge(v_done, G)
            pe.wait_ge(q_done, G)
            pe.wait_ge(qb_done, G)
            energies(0, 0)
            for_seqs(pe, attention)
            attn_transpose(B - 1)
            project_out(B - 1)
            norm_transpose(B - 1, B - 1)
            router(B - 1)

            pe.wait_ge(oh_done, 1)
            pe.wait_ge(const_done, 14)
            pe.matmul(bank[0][:, 0:B * E], before[:, :], onehotb[:, :, :].rearrange("p b e -> p (b e)"),
                      start=True, stop=False, skip_group_check=True)
            for b in range(B):
                last = pe.matmul(bank[0][:, (b + 1) * E:(B + 1) * E].rearrange("p (n e) -> p n e", e=E), ones[:, :],
                                 onehotb[:, b:b + 1, :].broadcast_to([P, B - b, E]),
                                 start=False, stop=(b == B - 1), skip_group_check=True)
            last.then_inc(rank_mm, 1)
            pe.wait_ge(rowhot_done, B)
            pe.wait_ge(tileval_done, 2)
            for b in range(B):
                last = pe.matmul(bank[1][:, 0:2 * TILES], row_hot[:, b, :],
                                 tile_val[:, b, :, :].rearrange("p s t -> p (s t)"), start=(b == 0), stop=(b == B - 1))
            last.then_inc(tok_mm, 1)
            pe.wait_ge(ld_w2, 16)
            pe.wait_ge(expert_done, 1)

            def rows_transpose(t, k, slot):
                pe.wait_ge(gathered[slot], gather_count(t, k))
                if k >= 2:
                    pe.wait_ge(xgt_done, t - 1)
                pe.transpose(bank[k % 2][:, 0:P], gat[slot][:, D:2 * D], ident[:, :]).then_inc(xgt_mm, 1)

            def up(t, k):
                pe.wait_ge(xgt_done, t + 1)
                pe.wait_ge(w1_ready[k % RING], gather_count(t, k))
                if k >= 2:
                    pe.wait_ge(hid_done, t - 1)
                for c in range(FC):
                    last = pe.matmul(bank[2 + k % 2][:, c * P:c * P + P], w1_ring[:, k % RING, c * P:c * P + P],
                                     xg_t[:, k % 2, :], start=(c == 0), stop=(c == FC - 1), skip_group_check=True)
                last.then_inc(up_mm, 1)

            def down(t, k):
                e = pe.value_load(expert[0:1, bass.ds(t, 1)], min_val=0, max_val=E - 1)
                pe.wait_ge(hid_done, t + 1)
                if k >= 2:
                    pe.wait_ge(yb_done, t - 1)
                for c in range(FC):
                    last = pe.matmul(bank[4 + k % 2][:, 0:D], hid[:, k % 2, c, :],
                                     w2_sb[:, bass.ds(e, 1), c, :].rearrange("p a d -> p (a d)"),
                                     start=(c == 0), stop=(c == FC - 1))
                last.then_inc(down_mm, 1)

            rows_transpose(0, 0, 0)
            up(0, 0)
            for t in range(1, PEEL):
                rows_transpose(t, t, t % RING)
                up(t, t)
                down(t - 1, t - 1)
            with pe.Fori(0, (TILES - PEEL) // RING) as i:
                for k in range(PEEL, PEEL + RING):
                    t = i * RING + k
                    rows_transpose(t, k, k % RING)
                    up(t, k)
                    down(t - 1, k - 1)
            down(TILES - 1, PEEL + RING - 1)

        NEWTON = 3
        RSTD_STEPS = 2 + 3 * NEWTON

        def inverse_std(y, half_var, t, var, stepped, n):
            dve = nc.vector
            count = n * RSTD_STEPS

            def then(ins):
                nonlocal count
                count = count + 1
                ins.then_inc(stepped, 1)
                dve.wait_ge(stepped, count)

            then(dve.tensor_scalar(half_var, var, EPS, 0.5, ALU.add, ALU.mult))
            then(dve.tensor_scalar(y.bitcast(I32), half_var.bitcast(I32), -0.5, float(0x5F3759DF - (1 << 22)),
                                   ALU.mult, ALU.add))
            for i in range(NEWTON):
                then(dve.tensor_tensor(t, y, half_var, ALU.mult))
                then(dve.tensor_tensor(t, t, y, ALU.mult))
                then(dve.scalar_tensor_tensor(y, t, 1.5, y, ALU.subtract, ALU.mult, reverse0=(i == NEWTON - 1)))

        @block.vector
        def _(dve):
            dve.memset(v_bd[:, CH // 2:CH, :, :, :], 0.0).then_inc(vbd_zero, 1)
            dve.wait_ge(wrep_mm, 1)
            dve.tensor_copy(wrep[:, :, :], bank[7][:, 0:3 * HV].rearrange("p (n d) -> p n d", n=3)).then_inc(wrep_done, 1)
            dve.wait_ge(wrep_done, 1)
            for n in range(3):
                last = dve.tensor_tensor(wbd[:, n, :, :], wrep[:, n:n + 1, 0:HD].broadcast_to([P, H, HD]),
                                         headmask[:, :].rearrange("p (h a) -> p h a", a=1).broadcast_to([P, H, HD]),
                                         ALU.mult)
            last.then_inc(wbd_done, 1)
            dve.tensor_copy(bv_cols[:, :], wrep[:, 1, HD:HV].broadcast_to([P, P])).then_inc(bvc_done, 1)
            dve.tensor_copy(identb[:, :], ident[:, :]).then_inc(const_done, 1)
            for g in range(G):
                js = slice(g * J, g * J + J)
                dve.wait_ge(ld_x[g], 16)
                for b in range(g * J, g * J + J):
                    dve.bn_stats(stats1[:, b, :], x_sb[:, b, :]).then_inc(st1_done, 1)
                for b in range(g * J, g * J + J):
                    dve.wait_ge(st1_done, b + 1)
                    dve.bn_aggr(mv1[:, b, :], stats1[:, b, :]).then_inc(mv1_done, 1)
                dve.wait_ge(mv1_done, (g + 1) * J)
                inverse_std(rstd1[:, js], half_var1[:, :], newton1[:, :], mv1[:, js, 1], rstd1_step, g)
                if g >= 2:
                    dve.wait_ge(xt_mm, g - 1)
                for j in range(J):
                    b = g * J + j
                    dve.tensor_scalar(xn1[:, g % 2, j, :], x_sb[:, b, :], mv1[:, b, 0:1], rstd1[:, b:b + 1],
                                      ALU.subtract, ALU.mult).then_inc(xn1_done, 1)
                dve.wait_ge(ctxt_mm, g + 1)
                dve.tensor_copy(ctx_t[:, js, :], bank[g % 2][:, 0:J * L].rearrange("p (j l) -> p j l", j=J)
                                ).then_inc(ctxt_done, 1)
                dve.wait_ge(v_mm, g + 1)
                dve.tensor_copy(v_src[:, :, js, 0:HD].rearrange("l h j d -> l j h d"),
                                bank[4 + g % 2][0:L, :].rearrange("l (j h d) -> l j h d", j=J, h=H)).then_inc(v_done, 1)
                dve.wait_ge(q_done, g + 1)
                dve.tensor_copy(q_tb[:, js, :], q_t[:, js, :]).then_inc(qb_done, 1)
                if g == 0:
                    dve.wait_ge(obias_mm, 1)
                    dve.wait_ge(ld_misc, 64)
                    dve.wait_ge(tanh_done, 1)
                    dve.scalar_tensor_tensor(out_bias[:, :], bo_bc[:, :], tanhs[:, 0:1], bank[3][:, 0:D],
                                             ALU.mult, ALU.add).then_inc(obias_done, 1)

            def row_max(b, k):
                dve.wait_ge(energy_mm, b + 1)
                full = [n for n, (h0, h1) in enumerate(E_HEADS) if h1 - h0 == PER_BANK]
                dve.tensor_reduce(emax[:, k % 2, 0:len(full) * PER_BANK].rearrange("p (n h) -> p n h", n=len(full)),
                                  ps_e[:, 0:len(full), 0:PER_BANK * L].rearrange("p n (h l) -> p n h l", l=L),
                                  AX, ALU.max)
                h0, h1 = E_HEADS[-1]
                dve.tensor_reduce(emax[:, k % 2, h0:h1], ps_e[:, E_BANKS - 1, 0:(h1 - h0) * L]
                                  .rearrange("p (h l) -> p h l", l=L), AX, ALU.max).then_inc(emax_done, 1)
                dve.wait_ge(emax_done, b + 1)
                if k >= 2:
                    dve.wait_ge(shiftt_mm, b - 1)
                dve.tensor_scalar(shift[:, k % 2, 0:H], emax[:, k % 2, :], -1.0, None, ALU.mult).then_inc(shift1_done, 1)
                dve.wait_ge(shift1_done, b + 1)
                dve.scalar_tensor_tensor(shift[:, k % 2, H:2 * H], emax[:, k % 2, :], -1.0, shift[:, k % 2, 0:H],
                                         ALU.mult, ALU.subtract).then_inc(shift_done, 1)

            def normalise(b):
                dve.wait_ge(pv_mm, b + 1)
                o = M1[:, 0:H * HV].rearrange("p (h d) -> p h d", h=H)
                dve.reciprocal(rden[:, :], o[:, :, HD]).then_inc(rden_done, 1)
                dve.wait_ge(rden_done, b + 1)
                if not (isinstance(b, int) and b == 0):
                    dve.wait_ge(at_mm, b)
                dve.tensor_tensor(attn[:, :].rearrange("p (h d) -> p h d", h=H), o[:, :, 0:HD],
                                  rden[:, :].rearrange("p (h a) -> p h a", a=1).broadcast_to([P, H, HD]),
                                  ALU.mult).then_inc(attn_done, 1)

            def residual_norm(b, k, row_wait):
                dve.wait_ge(wo_mm, b + 1)
                if row_wait is not None:
                    dve.wait_ge(row_store[k % 2], row_wait)
                x1 = rows[:, k % 2, 0:D]
                dve.tensor_tensor(x1, M0[:, 0:D], x_sb[:, bass.ds(b, 1), :].rearrange("p a d -> p (a d)"),
                                  ALU.add).then_inc(x1_done, 1)
                dve.wait_ge(x1_done, b + 1)
                dve.bn_stats(stats2[:, :], x1).then_inc(st2_done, 1)
                dve.wait_ge(st2_done, b + 1)
                detach(dve)
                dve.bn_aggr(mv2[:, :], stats2[:, :]).then_inc(mv2_done, 1)
                dve.wait_ge(mv2_done, b + 1)
                inverse_std(rstd2[:, :], half_var2[:, :], newton2[:, :], mv2[:, 1:2], rstd2_step, b)
                dve.tensor_scalar(rows[:, k % 2, D:2 * D], x1, mv2[:, 0:1], rstd2[:, 0:1],
                                  ALU.subtract, ALU.mult).then_inc(xn2_done, 1)

            def router_bias(b):
                dve.wait_ge(lg_mm, b + 1)
                dve.tensor_tensor(logits[:, bass.ds(b, 1), :].rearrange("p a e -> p (a e)"), M0[:, 0:E], sbias[:, :],
                                  ALU.add).then_inc(lg_done, 1)

            def attention(b, k):
                if k >= 1:
                    normalise(b - 1)
                dve.wait_ge(shiftt_mm, b + 1)
                if k >= 1:
                    dve.wait_ge(score_mm, b * T_BANKS)
                dve.tensor_copy(shift_t[:, :], M1.bitcast(BF16)[:, 0:P]).then_inc(shiftt_done, 1)
                if k >= 1:
                    wait = None
                    if k >= 3:
                        wait = (b - 1 - (k - 1) % 2) * 8
                    residual_norm(b - 1, k - 1, wait)
                if k + 1 < B:
                    row_max(b + 1, k + 1)
                if k >= 1:
                    router_bias(b - 1)

            dve.wait_ge(pad_zero, 2)
            dve.wait_ge(xres_done, G)
            dve.wait_ge(ld_router, 32)
            row_max(0, 0)
            for_seqs(dve, attention)
            normalise(B - 1)
            residual_norm(B - 1, B - 1, (B - 1 - (B - 1) % 2) * 8)
            router_bias(B - 1)

            done = [0]

            def step(ins):
                ins.then_inc(cs, 1)
                done[0] += 1
                dve.wait_ge(cs, done[0])

            def over_e(ap):
                return ap.rearrange("p (b a) -> p b a", a=1).broadcast_to([P, B, E])

            dve.wait_ge(lg_done, B)
            dve.wait_ge(const_done, 14)
            step(dve.tensor_reduce(lmax[:, :], logits[:, :, :], AX, ALU.max))
            dve.tensor_tensor(lsub[:, :, :], logits[:, :, :], over_e(lmax[:, :]), ALU.subtract).then_inc(lsub_done, 1)
            dve.wait_ge(lsub_done, 1)
            step(dve.scalar_tensor_tensor(is_max[:, :, :], lsub[:, :, :], 0.0,
                                          prefer_low[:, :].rearrange("p (a e) -> p a e", a=1).broadcast_to([P, B, E]),
                                          ALU.is_equal, ALU.mult))
            step(dve.tensor_reduce(pick[:, :], is_max[:, :, :], AX, ALU.max))
            step(dve.tensor_tensor(onehot[:, :, :], is_max[:, :, :], over_e(pick[:, :]), ALU.is_equal))
            dve.tensor_copy(onehotb[:, :, :], onehot[:, :, :]).then_inc(oh_done, 1)
            dve.wait_ge(lexp_done, 1)
            step(dve.tensor_reduce(lsum[:, :], lexp[:, :, :], AX, ALU.add))
            step(dve.reciprocal(lsum[:, :], lsum[:, :]))
            dve.tensor_scalar(scale_tok[:, :], lsum[:, :], tanhs[:, 1:2], None, ALU.mult).then_inc(scale_done, 1)
            dve.wait_ge(rank_mm, 1)
            count = bank[0][:, B * E:(B + 1) * E]
            step(dve.tensor_tensor(over[:, :, :], count.rearrange("p (e a) -> p e a", a=1).broadcast_to([P, E, B]),
                                   rank_step[:, :].rearrange("p (a b) -> p a b", a=1).broadcast_to([P, E, B]),
                                   ALU.is_gt))
            step(dve.tensor_reduce(n_tiles[:, :], over[:, :, :], AX, ALU.add))
            step(dve.tensor_tensor(base_prod[:, :, :], e_before[:, :, :],
                                   n_tiles[:, :].rearrange("p (a e) -> p a e", a=1).broadcast_to([P, E, E]), ALU.mult))
            step(dve.tensor_reduce(base[:, :], base_prod[:, :, :], AX, ALU.add))
            step(dve.tensor_tensor(end[:, :], base[:, :], n_tiles[:, :], ALU.add))
            step(dve.tensor_scalar(end[:, :], end[:, :], float(P), None, ALU.mult))
            step(dve.tensor_tensor(past[:, :, :], tile_start[:, :].rearrange("p (t a) -> p t a", a=1).broadcast_to([P, TILES, E]),
                                   end[:, :].rearrange("p (a e) -> p a e", a=1).broadcast_to([P, TILES, E]), ALU.is_ge))
            step(dve.tensor_reduce(expert_f[:, :], past[:, :, :], AX, ALU.add))
            dve.tensor_scalar(expert[:, :], expert_f[:, :], float(E - 1), None, ALU.min).then_inc(expert_done, 1)
            step(dve.scalar_tensor_tensor(slot_e[:, :, :], base[:, :].rearrange("p (a e) -> p a e", a=1).broadcast_to([P, B, E]),
                                          float(P), bank[0][:, 0:B * E].rearrange("p (b e) -> p b e", e=E),
                                          ALU.mult, ALU.add))
            step(dve.tensor_tensor(slot_m[:, :, :], slot_e[:, :, :], onehot[:, :, :], ALU.mult))
            step(dve.tensor_reduce(slot[:, :], slot_m[:, :, :], AX, ALU.add))
            step(dve.tensor_copy(slot_int[:, :], slot[:, :]))
            step(dve.tensor_scalar(slot_low[:, :], slot_int[:, :], P - 1, None, ALU.bitwise_and))
            step(dve.tensor_copy(slot_row[:, :], slot_low[:, :]))
            step(dve.tensor_tensor(slot_start[:, :], slot[:, :], slot_row[:, :], ALU.subtract))
            for b in range(B):
                dve.tensor_scalar(row_hot[:, b, :], iota_row[:, :], slot_row[:, b:b + 1], None,
                                  ALU.is_equal).then_inc(rowhot_done, 1)
            step(dve.tensor_tensor(tile_hot[:, :, :],
                                   tile_start[:, :].rearrange("p (a t) -> p a t", a=1).broadcast_to([P, B, TILES]),
                                   slot_start[:, :].rearrange("p (b a) -> p b a", a=1).broadcast_to([P, B, TILES]),
                                   ALU.is_equal))
            dve.tensor_scalar(tile_val[:, :, 0, :], tile_hot[:, :, :], iota_part[:, 0:1], None,
                              ALU.mult).then_inc(tileval_done, 1)
            dve.tensor_tensor(tile_val[:, :, 1, :], tile_hot[:, :, :],
                              seq_code[:, :].rearrange("p (b a) -> p b a", a=1).broadcast_to([P, B, TILES]),
                              ALU.mult).then_inc(tileval_done, 1)
            dve.wait_ge(tok_mm, 1)
            step(dve.tensor_scalar(tok_a[:, :], bank[1][:, TILES:2 * TILES], -float(P), float(NTOK), ALU.mult, ALU.add))
            dve.tensor_tensor(tok[:, :], tok_a[:, :], bank[1][:, 0:TILES], ALU.add).then_inc(tok_done, 1)

            dve.wait_ge(ld_b2, 16)

            def rows_copy(t, k):
                dve.wait_ge(xgt_mm, t + 1)
                if k >= 2:
                    dve.wait_ge(up_mm, t - 1)
                dve.tensor_copy(xg_t[:, k % 2, :], bank[k % 2][:, 0:P]).then_inc(xgt_done, 1)

            def combine(t, k, scatter_wait):
                e = dve.value_load(expert[0:1, bass.ds(t, 1)], min_val=0, max_val=E - 1)
                dve.wait_ge(down_mm, t + 1)
                dve.tensor_tensor(yb[:, k % 2, :], bank[4 + k % 2][:, 0:D],
                                  b2_bc[:, bass.ds(e, 1), :].rearrange("p a d -> p (a d)"), ALU.add).then_inc(yb_done, 1)
                dve.wait_ge(yb_done, t + 1)
                if scatter_wait is not None:
                    dve.wait_ge(scattered[k % 2], scatter_wait)
                g = gat[k % RING]
                dve.scalar_tensor_tensor(res[k % 2][:, :], yb[:, k % 2, :], g[:, 2 * D:ROW], g[:, 0:D],
                                         ALU.mult, ALU.add).then_inc(res_done, 1)

            def scatters_before(t, k):
                if isinstance(t, int):
                    return 16 * (t // 2) if t >= 2 else None
                return (t - (k % 2)) * 8

            for t in range(PEEL):
                rows_copy(t, t)
                if t >= 1:
                    combine(t - 1, t - 1, scatters_before(t - 1, t - 1))
            with dve.Fori(0, (TILES - PEEL) // RING) as i:
                for k in range(PEEL, PEEL + RING):
                    t = i * RING + k
                    rows_copy(t, k)
                    combine(t - 1, k - 1, scatters_before(t - 1, k - 1))
            combine(TILES - 1, PEEL + RING - 1, scatters_before(TILES - 1, 0))


_LAID = ["x", "ctx_1024", "g_xattn", "g_ffn", "L0_xattn_wq", "L0_xattn_bq", "L0_xattn_wk", "L0_xattn_bk",
         "L0_xattn_wv", "L0_xattn_bv", "L0_xattn_wo", "L0_xattn_bo", "L0_ffn_switch_w", "L0_ffn_switch_b",
         "L0_ffn_w1", "L0_ffn_b1", "L0_ffn_w2", "L0_ffn_b2"]
_TRANSPOSED = {"L0_xattn_wq", "L0_xattn_wk", "L0_xattn_wv", "L0_xattn_wo"}


def kernel(**inputs):
    import numpy as np
    import concourse.bacc as bacc
    from concourse.bass_utils import run_bass_kernel_spmd

    nc = bacc.Bacc("TRN2", target_bir_lowering=False, num_devices=1)
    arrays, args = {}, []
    for name in _LAID:
        a = np.asarray(inputs[name])
        if name in _TRANSPOSED:
            a = a.T
        if name == "L0_ffn_b1":
            a = a.reshape(-1, P).T
        a = np.ascontiguousarray(a)
        arrays[f"in_{name}"] = a
        args.append(nc.dram_tensor(f"in_{name}", a.shape, mybir.dt.from_np(a.dtype), kind="ExternalInput").ap())
    B, S, D = inputs["x"].shape
    out = nc.dram_tensor("out_rows", (B * S, D), F32, kind="ExternalOutput").ap()
    table = nc.dram_tensor("row_table", (B * S, 2 * D + 1), F32).ap()
    flamingo_layer(nc, *args, out, table)
    r = run_bass_kernel_spmd(nc, [arrays], core_ids=[0])
    return r.results[0]["out_rows"].reshape(B, S, D)
```

```python
import math
from contextlib import ExitStack

import concourse.bass as bass
from concourse import mybir

F32 = mybir.dt.float32
BF16 = mybir.dt.bfloat16
I32 = mybir.dt.int32
U32 = mybir.dt.uint32
ALU = mybir.AluOpType
ACT = mybir.ActivationFunctionType
AX = mybir.AxisListType.X

P = 128


def flamingo_layer(nc, x, ctx_in, g_xattn, g_ffn, w_heads, wo_t, bo,
                   switch_w, switch_b, w1, b1_t, w2, b2, out, table):
    B, S, D = x.shape
    L = ctx_in.shape[1]
    HD = w_heads.shape[0]
    H = D // HD
    E, _, F = w1.shape
    FC = F // P
    assert S == P and D == P and B % 4 == 0
    J = 4
    G = B // J
    NTOK = B * S
    TILES = NTOK // P + E - 1
    RING = 4
    GATHER_RING = 8
    PEEL = 7
    assert (TILES - PEEL) % GATHER_RING == 0
    HL = H * L
    HV = HD + 1
    HEAD_ROWS = P // 2
    TAIL_KEYS = L - HEAD_ROWS
    TAIL_HEADS = H // 2
    TAIL_ROWS = TAIL_HEADS * TAIL_KEYS
    CA = H // 2
    CH = CA + H // TAIL_HEADS
    assert 0 < TAIL_ROWS <= P
    W = 11
    assert W * HV >= 96
    W0 = [min(2 * c, H - W) for c in range(CA)] + [0, H - W]
    N0 = (H - W) // 2 + 1
    SCALE = float(D) ** -0.5
    EPS = 1e-5
    GUESS_SCALE = -0.5 * math.log(2.0) / 2 ** 23
    GUESS_BIAS = 0.5 * math.log(2.0) * (126 - 0.043)
    ROW = 2 * D + 1
    PER_BANK = 512 // L
    E_HEADS = [(h, min(h + PER_BANK, H)) for h in range(0, H, PER_BANK)]
    E_BANKS = len(E_HEADS)
    T_CHUNKS = [(0, 4), (4, 8), (8, CH)]
    T_BANKS = len(T_CHUNKS)
    assert E_BANKS + T_BANKS == 6 and CA == 8
    OWN = [(slice(0, N0), slice(0, N0 * W, W)),
           (slice(N0, CA), slice(N0 * W + 2 * N0 - (H - W), (CA - 1) * W + 2 * (CA - 1) - (H - W) + 1, W + 2))]

    with ExitStack() as ctx:
        def sb(name, shape, dt=F32):
            return ctx.enter_context(nc.sbuf_tensor(name, shape, dt))

        def sem(name):
            return ctx.enter_context(nc.semaphore(name))

        ident = sb("ident", [P, P])
        identb = sb("identb", [P, P], BF16)
        rep = sb("rep", [HD, P])
        headmask = sb("headmask", [P, H])
        headsel = sb("headsel", [P, HL], BF16)
        sel = sb("sel", [P, H])
        tailmask = sb("tailmask", [P, TAIL_HEADS])
        zero_col, guess_bias = sb("zero_col", [P, 1]), sb("guess_bias", [P, 1])
        before = sb("before", [P, P], BF16)
        ones = sb("ones", [P, P], BF16)
        iota_row = sb("iota_row", [P, P], BF16)
        iota_part = sb("iota_part", [P, 1])
        tile_start = sb("tile_start", [P, TILES], BF16)
        tile_no = sb("tile_no", [1, TILES])
        rank_step = sb("rank_step", [P, B])
        prefer_low = sb("prefer_low", [P, E])
        seq_code = sb("seq_code", [P, B], BF16)
        e_before = sb("e_before", [P, E, E])
        gates = sb("gates", [P, 2])
        tanhs = sb("tanhs", [P, 2])
        w_small = sb("w_small", [HD, 3, HV])
        wrep = sb("wrep", [P, 3, HV])
        wbd = sb("wbd", [P, 3, H, HD])
        bv_cols = sb("bv_cols", [P, P])
        wo_sb = sb("wo_sb", [P, D])
        wo_g = sb("wo_g", [P, D])
        bo_bc = sb("bo_bc", [P, D])
        out_bias = sb("out_bias", [P, D])
        sw_sb = sb("sw_sb", [P, E])
        sbias = sb("sbias", [P, E])
        w2_sb = sb("w2_sb", [P, E, FC, D])
        b1_sb = sb("b1_sb", [P, E, FC])
        b2_bc = sb("b2_bc", [P, E, D])
        ctx_sb = sb("ctx_sb", [L, B, D])
        ctx_t = sb("ctx_t", [P, B, P + TAIL_ROWS])
        k_t = sb("k_t", [P, B, L])
        x_sb = sb("x_sb", [P, B, D])
        stats1 = sb("stats1", [P, B, 6])
        mv1 = sb("mv1", [P, B, 2])
        guess1, half_var1, newton1, rstd1 = (
            sb(n, [P, B]) for n in ("guess1", "half_var1", "newton1", "rstd1"))
        guess2, half_var2, newton2 = (sb(n, [P, 1]) for n in ("guess2", "half_var2", "newton2"))
        w1_ring = sb("w1_ring", [P, RING, F])
        xn1 = w1_ring[:, :, :].rearrange("p r f -> p (r f)").rearrange("p (b d) -> p b d", b=B)
        xn1_t = sb("xn1_t", [P, 2, J, P])
        q_t = sb("q_t", [P, B, P])
        q_tb = sb("q_tb", [P, B, P], BF16)
        v_bd = sb("v_bd", [P, CH * W, B, HV])
        k_bd = sb("k_bd", [P, 2, HL])
        k_bdb = sb("k_bdb", [P, 2, HL], BF16)
        emax = sb("emax", [P, 2, H])
        shift = sb("shift", [P, 2, P], BF16)
        shift_t = sb("shift_t", [P, P], BF16)
        probs = sb("probs", [P, CH * P])
        rden = sb("rden", [P, H])
        attn = sb("attn", [P, D])
        attn_t = sb("attn_t", [P, P])
        stats2 = sb("stats2", [P, 6])
        mv2 = sb("mv2", [P, 2])
        rstd2 = sb("rstd2", [P, 1])
        rows = sb("rows", [P, 2, 2 * D])
        xn2_t = sb("xn2_t", [P, P])
        logits = sb("logits", [P, B, E])
        gelu_warm = sb("gelu_warm", [P, 1])
        lmax = sb("lmax", [P, B])
        lsub = sb("lsub", [P, B, E])
        lexp = sb("lexp", [P, B, E])
        lsum = sb("lsum", [P, B])
        scale_tok = sb("scale_tok", [P, B])
        is_max = sb("is_max", [P, B, E])
        pick = sb("pick", [P, B])
        onehotb = sb("onehotb", [P, B, E], BF16)
        over = sb("over", [P, E, B])
        n_tiles = sb("n_tiles", [P, E])
        base_prod = sb("base_prod", [P, E, E])
        base = sb("base", [P, E])
        end = sb("end", [1, E])
        slot_e = sb("slot_e", [P, B, E])
        slot_m = sb("slot_m", [P, B, E])
        slot = sb("slot", [P, B])
        slot_int = sb("slot_int", [P, B], I32)
        slot_low = sb("slot_low", [P, B], I32)
        slot_row = sb("slot_row", [P, B])
        slot_start = sb("slot_start", [P, B], BF16)
        row_hot = sb("row_hot", [P, B, P], BF16)
        tile_hot = sb("tile_hot", [P, B, TILES], BF16)
        tile_val = sb("tile_val", [P, B, 2, TILES], BF16)
        past = sb("past", [1, TILES, E])
        expert_f = sb("expert_f", [1, TILES])
        expert = sb("expert", [1, TILES], I32)
        tok_a = sb("tok_a", [P, TILES])
        tok = sb("tok", [P, TILES], U32)
        hid = sb("hid", [P, 2, FC, P])
        gat = [ctx_t[:, :, :].rearrange("p b l -> p (b l)")[:, i * ROW:(i + 1) * ROW] for i in range(GATHER_RING)]
        xg_t = sb("xg_t", [P, 2, P])
        yb = sb("yb", [P, 2, D])
        res = [sb(f"res{i}", [P, D]) for i in range(RING)]

        pe_bank = [ctx.enter_context(nc.psum_tensor(f"ps{i}", [P, 512], F32)) for i in range(2)]
        ps_e = ctx.enter_context(nc.psum_tensor("ps_e", [P, E_BANKS, 512], F32))
        ps_t = ctx.enter_context(nc.psum_tensor("ps_t", [P, T_BANKS, 512], F32))
        bank = [ps_e[:, i, :] for i in range(E_BANKS)] + [ps_t[:, i, :] for i in range(T_BANKS)] \
            + [pe_bank[0][:, :], pe_bank[1][:, :]]
        M0, M1 = bank[6], bank[7]

        ld_small, ld_ctx, ld_x, ld_misc = sem("ld_small"), [sem(f"ld_ctx{g}") for g in range(G)], \
            [sem(f"ld_x{g}") for g in range(G)], sem("ld_misc")
        ld_router, ld_w2, ld_b1, ld_b2 = sem("ld_router"), sem("ld_w2"), sem("ld_b1"), sem("ld_b2")
        passed = sem("passed")
        zeroed = sem("zeroed")
        const_done, identb_done = sem("const_done"), sem("identb_done")
        mask_step = sem("mask_step")
        vbd_zero = sem("vbd_zero")
        cols_ready = sem("cols_ready")
        sel_done = sem("sel_done")
        v_ones = sem("v_ones")
        pad_zero = sem("pad_zero")
        wrep_mm = sem("wrep_mm")
        wrep_done = sem("wrep_done")
        wbd_done = sem("wbd_done")
        tanh_done = sem("tanh_done")
        wog_done = sem("wog_done")
        bvc_done = sem("bvc_done")
        obias_mm = sem("obias_mm")
        obias_done = sem("obias_done")
        xres_done = sem("xres_done")
        ctxt_mm, ctxt_done, ctxtail_done = sem("ctxt_mm"), sem("ctxt_done"), sem("ctxtail_done")
        k_mm, k_done = sem("k_mm"), sem("k_done")
        v_mm, vtail_mm, v_done, vtail_done = sem("v_mm"), sem("vtail_mm"), sem("v_done"), sem("vtail_done")
        st1_done, mv1_done, rstd1_step, xn1_done = sem("st1_done"), sem("mv1_done"), sem("rstd1_step"), sem("xn1_done")
        guess1_done = sem("guess1_done")
        xt_mm, xt_done = sem("xt_mm"), sem("xt_done")
        q_mm, q_done, qb_done = sem("q_mm"), sem("q_done"), sem("qb_done")
        keys_ready, keysb_ready = sem("keys_ready"), sem("keysb_ready")
        energy_mm, emax_done, shift1_done, shift_done = sem("energy_mm"), sem("emax_done"), sem("shift1_done"), sem("shift_done")
        shiftt_mm, shiftt_done = sem("shiftt_mm"), sem("shiftt_done")
        score_mm, exp_done = sem("score_mm"), sem("exp_done")
        pv_mm, rden_done, attn_done = sem("pv_mm"), sem("rden_done"), sem("attn_done")
        at_mm, at_done = sem("at_mm"), sem("at_done")
        wo_mm, x1_done, st2_done, mv2_done, hv2_done, rstd2_step, xn2_done = (
            sem("wo_mm"), sem("x1_done"), sem("st2_done"), sem("mv2_done"), sem("hv2_done"), sem("rstd2_step"), sem("xn2_done"))
        guess2_done = sem("guess2_done")
        x2t_mm, x2t_done, lg_mm, lg_done = sem("x2t_mm"), sem("x2t_done"), sem("lg_mm"), sem("lg_done")
        row_store = [sem("row_store0"), sem("row_store1")]
        cs = sem("route_step")
        lsub_done, lexp_done, scale_done, scale_store = sem("lsub_done"), sem("lexp_done"), sem("scale_done"), sem("scale_store")
        oh_done, rank_mm, rowhot_done, tileval_done, tok_mm = (
            sem("oh_done"), sem("rank_mm"), sem("rowhot_done"), sem("tileval_done"), sem("tok_mm"))
        base_done = sem("base_done")
        tok_done, expert_done = sem("tok_done"), sem("expert_done")
        gat_zero = sem("gat_zero")
        gathered = [sem(f"gathered{i}") for i in range(GATHER_RING)]
        w1_ready = [sem(f"w1_ready{i}") for i in range(RING)]
        xgt_mm, xgt_done = sem("xgt_mm"), sem("xgt_done")
        up_mm, hid_done, down_mm = sem("up_mm"), sem("hid_done"), sem("down_mm")
        yb_done, res_done = sem("yb_done"), sem("res_done")
        scattered = [sem(f"scattered{i}") for i in range(RING)]

        block = ctx.enter_context(nc.Block())

        def for_tiles(eng, tile_step):
            for t in range(PEEL):
                tile_step(t, t)
            with eng.Fori(0, (TILES - PEEL) // GATHER_RING) as i:
                for k in range(PEEL, PEEL + GATHER_RING):
                    tile_step(i * GATHER_RING + k, k)

        def for_seqs(eng, seq_step):
            for b in range(3):
                seq_step(b, b)
            with eng.Fori(0, (B - 6) // 2) as i:
                seq_step(i * 2 + 3, 3)
                seq_step(i * 2 + 4, 4)
            for b in range(B - 3, B):
                seq_step(b, b)

        def detach(eng):
            eng.sem_inc(passed, 1)

        def chunk_rows(c):
            return (P, c * P) if c < CA else (TAIL_ROWS, CA * P + (c - CA) * TAIL_ROWS)

        def add_out_bias(pool, g):
            js = slice(g * J, g * J + J)
            pool.tensor_tensor(x_sb[:, js, :], x_sb[:, js, :],
                               out_bias[:, :].rearrange("p (a d) -> p a d", a=1).broadcast_to([P, J, D]),
                               ALU.add).then_inc(xres_done, 1)

        v_flat = v_bd[:, :, :, :].rearrange("p h b d -> p (h b d)")
        ZERO_SPLIT = (3000, 4500, 5400, 6300, 7200)

        KEY_PARTS = ((slice(0, CA * P), slice(0, HEAD_ROWS)), (slice(CA * P, HL), slice(HEAD_ROWS, L)))

        def round_keys(act, b, k):
            act.wait_ge(keys_ready, b + 1)
            for part, keys in KEY_PARTS:
                last = act.activation(k_bdb[:, k % 2, :].rearrange("p (h l) -> p h l", h=H)[:, :, keys],
                                      k_bd[:, k % 2, part].rearrange("p (h l) -> p h l", h=H), ACT.Copy)
            last.then_inc(keysb_ready, 1)

        def build_keys(pool, b, k):
            src = k_t[:, bass.ds(b, 1), :].broadcast_to([P, H, L])
            mask = headmask[:, :].rearrange("p (h a) -> p h a", a=1).broadcast_to([P, H, L])
            for part, keys in KEY_PARTS:
                last = nc.gpsimd.tensor_tensor(k_bd[:, k % 2, part].rearrange("p (h l) -> p h l", h=H), src[:, :, keys],
                                               mask[:, :, keys], ALU.mult)
            last.then_inc(keys_ready, 1)

        def fill_count(t, k, ring):
            if isinstance(t, int):
                return 16 * (t // ring + 1)
            return (t - (k % ring)) * (16 // ring) + 16

        @block.sync
        def _(sp):
            def load_x(g):
                js = slice(g * J, g * J + J)
                sp.dma_start(x_sb[:, js, :], x[js].rearrange("b s d -> s b d")).then_inc(ld_x[g], 16)

            for g in range(G):
                js = slice(g * J, g * J + J)
                sp.dma_start(ctx_sb[:, js, :], ctx_in[js].rearrange("b l d -> l b d")).then_inc(ld_ctx[g], 16)
                if g == 0:
                    sp.dma_start(w_small[:, :, :], w_heads).then_inc(ld_small, 16)
                else:
                    load_x(g - 1)
            load_x(G - 1)
            sp.dma_start(gates[:, 0:1], g_xattn.rearrange("(a b) -> a b", a=1).broadcast_to([P, 1])).then_inc(ld_misc, 16)
            sp.dma_start(gates[:, 1:2], g_ffn.rearrange("(a b) -> a b", a=1).broadcast_to([P, 1])).then_inc(ld_misc, 16)
            sp.dma_start(wo_sb[:, :], wo_t).then_inc(ld_misc, 16)
            sp.dma_start(bo_bc[:, :], bo.rearrange("(a d) -> a d", a=1).broadcast_to([P, D])).then_inc(ld_misc, 16)
            sp.dma_start(sw_sb[:, :], switch_w).then_inc(ld_router, 16)
            sp.dma_start(sbias[:, :], switch_b.rearrange("(a d) -> a d", a=1).broadcast_to([P, E])).then_inc(ld_router, 16)
            sp.dma_start(w2_sb[:, :, :, :], w2.rearrange("e (c p) d -> p e c d", p=P)).then_inc(ld_w2, 16)
            sp.dma_start(b1_sb[:, :, :], b1_t.rearrange("p (e c) -> p e c", e=E)).then_inc(ld_b1, 16)
            sp.dma_start(b2_bc[:, :, :].rearrange("p e d -> p (e d)"),
                         b2.rearrange("(a e) d -> a (e d)", a=1).broadcast_to([P, E * D])
                         ).then_inc(ld_b2, 16)

            def store_rows(b, k):
                sp.wait_ge(xn2_done, b + 1)
                sp.dma_start(table[bass.ds(b * P, P), 0:2 * D], rows[:, k % 2, :]).then_inc(row_store[k % 2], 16)

            for_seqs(sp, store_rows)
            sp.wait_ge(scale_done, 1)
            sp.dma_start(table.rearrange("(b p) r -> p b r", p=P)[:, :, 2 * D:ROW],
                         scale_tok[:, :].rearrange("p (b a) -> p b a", a=1), allow_slow_non_contiguous=True).then_inc(scale_store, 16)

            sp.wait_ge(expert_done, 1)

            def load_w1(t, k):
                if k >= RING:
                    sp.wait_ge(up_mm, t - RING + 1)
                e = sp.value_load(expert[0:1, bass.ds(t, 1)], min_val=0, max_val=E - 1)
                sp.dma_start(w1_ring[:, k % RING, :], w1[bass.ds(e, 1)].rearrange("e p f -> p (e f)")
                             ).then_inc(w1_ready[k % RING], 16)

            for_tiles(sp, load_w1)

        @block.gpsimd
        def _(pool):
            pool.memset(zero_col[:, :], 0.0).then_inc(cols_ready, 1)
            pool.memset(guess_bias[:, :], GUESS_BIAS).then_inc(cols_ready, 1)
            pool.memset(rep[:, :], 0.0).then_inc(zeroed, 1)
            pool.memset(ident[:, :], 0.0).then_inc(zeroed, 1)
            pool.memset(headmask[:, :], 1.0).then_inc(zeroed, 1)
            pool.memset(tailmask[:, :], 1.0).then_inc(zeroed, 1)
            pool.wait_ge(zeroed, 4)
            pool.affine_select(ident[:, :], ident[:, :], pattern=[[-1, P]], compare_op=ALU.not_equal,
                               fill=1.0, base=0, channel_multiplier=1).then_inc(const_done, 1)
            pool.affine_select(rep[:, :].rearrange("i (h j) -> i h j", h=H), rep[:, :].rearrange("i (h j) -> i h j", h=H),
                               pattern=[[0, H], [-1, HD]], compare_op=ALU.not_equal,
                               fill=1.0, base=0, channel_multiplier=1).then_inc(const_done, 1)
            for n, (mask, rows_each, heads) in enumerate(((headmask, HD, H), (tailmask, TAIL_KEYS, TAIL_HEADS))):
                pool.affine_select(mask[:, :], mask[:, :], pattern=[[-rows_each, heads]], compare_op=ALU.is_ge,
                                   fill=0.0, base=0, channel_multiplier=1).then_inc(mask_step, 1)
                pool.wait_ge(mask_step, n + 1)
                pool.affine_select(mask[:, :], mask[:, :], pattern=[[rows_each, heads]], compare_op=ALU.is_ge,
                                   fill=0.0, base=rows_each - 1, channel_multiplier=-1).then_inc(const_done, 1)
            pool.memset(v_flat[:, ZERO_SPLIT[-1]:], 0.0).then_inc(vbd_zero, 1)
            pool.memset(shift[:, :, :], 0.0).then_inc(pad_zero, 1)
            pool.wait_ge(vbd_zero, 1 + len(ZERO_SPLIT))
            pool.wait_ge(pad_zero, 1)
            for odd in range(2):
                for n, (_, own) in enumerate(OWN):
                    if odd or n:
                        pool.wait_ge(v_ones, 2 * odd + n)
                    cols = slice(own.start + odd, own.stop + odd, own.step)
                    pool.memset(v_bd[odd * HEAD_ROWS:(odd + 1) * HEAD_ROWS, cols, :, HD:HV], 1.0).then_inc(v_ones, 1)
            for n in range(2):
                pool.wait_ge(v_ones, 4 + n)
                h0 = (CA + n) * W + n * TAIL_HEADS - W0[CA + n]
                pool.tensor_copy(v_bd[0:TAIL_ROWS, h0:h0 + TAIL_HEADS, :, HD],
                                 tailmask[0:TAIL_ROWS, :].rearrange("p (h a) -> p h a", a=1)
                                 .broadcast_to([TAIL_ROWS, TAIL_HEADS, B])).then_inc(v_ones, 1)
            pool.wait_ge(v_ones, 6)
            pool.wait_ge(k_done, 1)
            for b in range(2):
                build_keys(pool, b, b)
            pool.wait_ge(obias_done, 1)
            pool.wait_ge(xn1_done, J)
            add_out_bias(pool, 0)

            def keys_ahead(b, k):
                for g in range(1, G):
                    if k == min(g, 2):
                        pool.wait_ge(xn1_done, (g + 1) * J)
                        add_out_bias(pool, g)
                if k + 2 < B:
                    pool.wait_ge(score_mm, T_BANKS * b + T_BANKS)
                    if k + 2 == J:
                        pool.wait_ge(k_done, G)
                    build_keys(pool, b + 2, k + 2)

            for_seqs(pool, keys_ahead)

            pool.iota(iota_row[:, :], pattern=[[1, P]], base=0, channel_multiplier=0,
                      allow_small_or_imprecise_dtypes=True).then_inc(const_done, 1)
            pool.iota(iota_part[:, :], pattern=[[1, 1]], base=0, channel_multiplier=1,
                      allow_small_or_imprecise_dtypes=True).then_inc(const_done, 1)
            pool.iota(tile_no[:, :], pattern=[[1, TILES]], base=0, channel_multiplier=0,
                      allow_small_or_imprecise_dtypes=True).then_inc(const_done, 1)
            pool.iota(tile_start[:, :], pattern=[[P, TILES]], base=0, channel_multiplier=0,
                      allow_small_or_imprecise_dtypes=True).then_inc(const_done, 1)
            pool.iota(rank_step[:, :], pattern=[[P, B]], base=0, channel_multiplier=0,
                      allow_small_or_imprecise_dtypes=True).then_inc(const_done, 1)
            pool.iota(prefer_low[:, :], pattern=[[-1, E]], base=E, channel_multiplier=0,
                      allow_small_or_imprecise_dtypes=True).then_inc(const_done, 1)
            pool.iota(seq_code[:, :], pattern=[[-1, B]], base=B, channel_multiplier=0,
                      allow_small_or_imprecise_dtypes=True).then_inc(const_done, 1)
            pool.memset(ones[:, :], 1.0).then_inc(const_done, 1)
            pool.memset(before[:, :], 1.0).then_inc(zeroed, 1)
            pool.memset(e_before[:, :, :], 1.0).then_inc(zeroed, 1)
            pool.wait_ge(zeroed, 6)
            pool.affine_select(before[:, :], before[:, :], pattern=[[1, P]], compare_op=ALU.is_ge, fill=0.0,
                               base=-1, channel_multiplier=-1).then_inc(const_done, 1)
            pool.affine_select(e_before[:, :, :], e_before[:, :, :], pattern=[[1, E], [-1, E]], compare_op=ALU.is_ge,
                               fill=0.0, base=-1, channel_multiplier=0).then_inc(const_done, 1)
            for i in range(GATHER_RING):
                pool.memset(gat[i], 0.0).then_inc(gat_zero, 1)
            pool.wait_ge(gat_zero, GATHER_RING)
            pool.wait_ge(scale_store, 16)
            for i in range(2):
                pool.wait_ge(row_store[i], 16 * (B // 2))
            pool.wait_ge(tok_done, 1)

            def gather(t):
                if t >= GATHER_RING:
                    pool.wait_ge(res_done, t - GATHER_RING + 1)
                slot = t % GATHER_RING
                pool.indirect_dma_start(
                    out=gat[slot], out_offset=None, in_=table[:, :],
                    in_offset=bass.IndirectOffsetOnAxis(ap=tok[:, t:t + 1], axis=0),
                    bounds_check=NTOK - 1, oob_is_err=False).then_inc(gathered[slot], 16)

            def scatter(t):
                pool.wait_ge(res_done, t + 1)
                pool.indirect_dma_start(
                    out=out, out_offset=bass.IndirectOffsetOnAxis(ap=tok[:, t:t + 1], axis=0),
                    in_=res[t % RING][:, :], in_offset=None,
                    bounds_check=NTOK - 1, oob_is_err=False).then_inc(scattered[t % RING], 16)

            for t in range(GATHER_RING):
                gather(t)
            for t in range(TILES):
                scatter(t)
                if t + GATHER_RING < TILES:
                    gather(t + GATHER_RING)
            for i in range(RING):
                pool.wait_ge(scattered[i], 16 * len(range(i, TILES, RING)))

        @block.scalar
        def _(act):
            def zero(n):
                cols = slice(ZERO_SPLIT[n], ZERO_SPLIT[n + 1])
                act.activation(v_flat[:, cols], zero_col[:, :].broadcast_to([P, cols.stop - cols.start]),
                               ACT.Copy).then_inc(vbd_zero, 1)

            def first_values(g):
                js = slice(g * J, g * J + J)
                act.wait_ge(v_mm, g + 1)
                act.wait_ge(vbd_zero, 1 + len(ZERO_SPLIT))
                for odd in range(2):
                    half = slice(odd * HEAD_ROWS, (odd + 1) * HEAD_ROWS)
                    pairs = bank[g][half, :].rearrange("l (j c o d) -> l j c o d", j=J, c=CA, o=2)
                    for chunks, own in OWN:
                        cols = slice(own.start + odd, own.stop + odd, own.step)
                        last = act.activation(v_bd[half, cols, js, 0:HD].rearrange("l c j d -> l j c d"),
                                              pairs[:, :, chunks, odd, :], ACT.Copy)
                last.then_inc(v_done, 1)

            def norms(g):
                act.wait_ge(xt_mm, g + 1)
                if g >= 2:
                    act.wait_ge(q_mm, g - 1)
                act.activation(xn1_t[:, g % 2, :, :].rearrange("p j s -> p (j s)"), bank[6][:, :],
                               ACT.Copy).then_inc(xt_done, 1)

            def queries(g):
                js = slice(g * J, g * J + J)
                act.wait_ge(q_mm, g + 1)
                for q, done in ((q_t, q_done), (q_tb, qb_done)):
                    act.activation(q[:, js, :].rearrange("p j s -> p (j s)"), bank[7][:, :],
                                   ACT.Identity, bias=wrep[:, 2, HD:HV]).then_inc(done, 1)

            act.wait_ge(cols_ready, 2)
            zero(0)
            for g in range(G):
                act.wait_ge(ctxt_mm, g + 1)
                keys = bank[g][:, 0:J * L].rearrange("p (j a l) -> p j a l", j=J, a=1)
                act.activation(ctx_t[:, g * J:g * J + J, 0:P].rearrange("p j (a l) -> p j a l", a=2),
                               keys[:, :, :, 0:HEAD_ROWS].broadcast_to([P, J, 2, HEAD_ROWS]), ACT.Copy).then_inc(ctxt_done, 1)
                if g + 1 < G:
                    zero(g + 1)
            act.wait_ge(wrep_done, 1)
            for g in range(G):
                act.wait_ge(k_mm, g + 1)
                act.activation(k_t[:, g * J:g * J + J, :], bank[4 + g % 2][:, 0:J * L].rearrange("p (j l) -> p j l", j=J),
                               ACT.Identity, bias=wrep[:, 0, HD:HV]).then_inc(k_done, 1)
            act.wait_ge(ld_misc, 64)
            act.activation(tanhs[:, :], gates[:, :], ACT.Tanh).then_inc(tanh_done, 1)
            act.wait_ge(tanh_done, 1)
            act.activation(wo_g[:, :], wo_sb[:, :], ACT.Copy, scale=tanhs[:, 0:1]).then_inc(wog_done, 1)
            act.wait_ge(rstd1_step, 1)
            act.activation(guess1[:, :], half_var1[:, :].bitcast(I32), ACT.Exp, scale=GUESS_SCALE,
                           bias=guess_bias[:, :]).then_inc(guess1_done, 1)
            first_values(0)
            first_values(1)
            norms(0)
            first_values(2)
            queries(0)
            norms(1)
            first_values(3)
            queries(1)
            norms(2)
            queries(2)
            norms(3)
            queries(3)
            round_keys(act, 0, 0)

            def copy_norms(b):
                act.wait_ge(x2t_mm, b + 1)
                act.activation(xn2_t[:, :], M0[:, 0:P], ACT.Copy).then_inc(x2t_done, 1)

            def copy_attn(b):
                act.wait_ge(at_mm, b + 1)
                act.activation(attn_t[:, :], M0[:, 0:P], ACT.Copy).then_inc(at_done, 1)

            def guess_inverse_std(b):
                act.wait_ge(hv2_done, b + 1)
                act.activation(guess2[:, :], half_var2[:, :].bitcast(I32), ACT.Exp, scale=GUESS_SCALE,
                               bias=guess_bias[:, :]).then_inc(guess2_done, 1)

            def attention(b, k):
                if k + 1 < B:
                    round_keys(act, b + 1, k + 1)
                if k >= 2:
                    copy_norms(b - 2)
                if k >= 1:
                    copy_attn(b - 1)
                for n, (c0, c1) in enumerate(T_CHUNKS):
                    act.wait_ge(score_mm, b * T_BANKS + n + 1)
                    if n == 0 and k >= 1:
                        act.wait_ge(pv_mm, b)
                    rows_used = P if c1 <= CA else TAIL_ROWS
                    act.activation(probs[0:rows_used, c0 * P:c1 * P], bank[3 + n][0:rows_used, 0:(c1 - c0) * P], ACT.Exp,
                                   scale=SCALE).then_inc(exp_done, 1)
                if k >= 1:
                    guess_inverse_std(b - 1)

            for_seqs(act, attention)
            copy_norms(B - 2)
            copy_attn(B - 1)
            guess_inverse_std(B - 1)
            copy_norms(B - 1)
            act.wait_ge(lsub_done, 1)
            act.activation(lexp[:, :, :], lsub[:, :, :], ACT.Exp).then_inc(lexp_done, 1)
            act.activation(gelu_warm[:, :], zero_col[:, :], ACT.Gelu_apprx_tanh)
            act.wait_ge(ld_b1, 16)
            act.wait_ge(expert_done, 1)

            def gelu(t, k):
                e = act.value_load(expert[0:1, bass.ds(t, 1)], min_val=0, max_val=E - 1)
                if k >= 2:
                    act.wait_ge(down_mm, t - 1)
                for c in range(FC):
                    act.wait_ge(up_mm, t + 1) if c == 0 else None
                    last = act.activation(hid[:, k % 2, c, :], bank[2 + k % 2][:, c * P:c * P + P], ACT.Gelu_apprx_tanh,
                                          bias=b1_sb[:, bass.ds(e, 1), c])
                last.then_inc(hid_done, 1)

            for_tiles(act, gelu)

        @block.tensor
        def _(pe):
            pe.wait_ge(const_done, 2)
            wbd_k, wbd_v, wbd_q = (wbd[:, n, :, :].rearrange("p h d -> p (h d)") for n in range(3))

            def keys(g):
                pe.wait_ge(ctxt_done, g + 1)
                pe.wait_ge(ctxtail_done, g + 1)
                if g >= 2:
                    pe.wait_ge(k_done, g - 1)
                pe.matmul(bank[4 + g % 2][:, 0:J * L], wbd_k, ctx_t[:, g * J:g * J + J, HEAD_ROWS:HEAD_ROWS + L],
                          start=True, stop=True).then_inc(k_mm, 1)

            def values(g):
                for j in range(J):
                    last = pe.matmul(bank[g][:, j * D:j * D + D], ctx_t[:, g * J + j, 0:P], wbd_v,
                                     start=(j == 0), stop=(j == J - 1), skip_group_check=True)
                last.then_inc(v_mm, 1)
                if g < 2:
                    pe.wait_ge(k_done, g + 3)
                else:
                    pe.wait_ge(vtail_done, g - 1)
                for j in range(J):
                    last = pe.matmul(bank[4 + g % 2][0:TAIL_ROWS, j * D:j * D + D], ctx_t[:, g * J + j, P:P + TAIL_ROWS],
                                     wbd_v, start=(j == 0), stop=(j == J - 1), skip_group_check=True)
                last.then_inc(vtail_mm, 1)

            def norms(g):
                pe.wait_ge(xn1_done, (g + 1) * J)
                if g >= 1:
                    pe.wait_ge(xt_done, g)
                for j in range(J):
                    last = pe.transpose(bank[6][:, j * P:j * P + P], xn1[:, g * J + j, :], ident[:, :])
                last.then_inc(xt_mm, 1)

            def queries(g):
                pe.wait_ge(xt_done, g + 1)
                if g == 0:
                    pe.wait_ge(obias_done, 1)
                else:
                    pe.wait_ge(qb_done, g)
                pe.matmul(bank[7][:, :], wbd_q, xn1_t[:, g % 2, :, :].rearrange("p j s -> p (j s)"),
                          start=True, stop=True).then_inc(q_mm, 1)

            for g in range(G):
                pe.wait_ge(ld_ctx[g], 16)
                for j in range(J):
                    last = pe.transpose(bank[g][:, j * L:j * L + L], ctx_sb[:, g * J + j, :], ident[0:L, 0:L])
                last.then_inc(ctxt_mm, 1)
                if g == 0:
                    pe.wait_ge(ld_small, 16)
                    pe.matmul(bank[7][:, 0:3 * HV], rep[:, :], w_small[:, :, :].rearrange("p n d -> p (n d)"),
                              start=True, stop=True).then_inc(wrep_mm, 1)
                    pe.wait_ge(wbd_done, 1)
                else:
                    keys(g - 1)
            keys(G - 1)
            values(0)
            values(1)
            pe.wait_ge(bvc_done, 1)
            pe.wait_ge(wog_done, 1)
            pe.matmul(bank[7][:, 0:D], bv_cols[:, :], wo_g[:, :], start=True, stop=True).then_inc(obias_mm, 1)
            norms(0)
            values(2)
            queries(0)
            norms(1)
            values(3)
            queries(1)
            norms(2)
            queries(2)
            norms(3)
            queries(3)

            def energies(b, k):
                pe.wait_ge(keysb_ready, b + 1)
                for n, (h0, h1) in enumerate(E_HEADS):
                    last = pe.matmul(bank[n][:, 0:(h1 - h0) * L],
                                     q_tb[:, bass.ds(b, 1), :].rearrange("p a s -> p (a s)"),
                                     k_bdb[:, k % 2, h0 * L:h1 * L], start=True, stop=True)
                last.then_inc(energy_mm, 1)

            def scores(b, k, n):
                c0, c1 = T_CHUNKS[n]
                if k >= 1:
                    pe.wait_ge(exp_done, (b - 1) * T_BANKS + n + 1)
                for c in range(c0, c1):
                    m, at = chunk_rows(c)
                    pe.matmul(bank[3 + n][0:m, (c - c0) * P:(c - c0) * P + P], k_bd[:, k % 2, at:at + m],
                              q_t[:, bass.ds(b, 1), :].rearrange("p a s -> p (a s)"), start=(c == c0), stop=False,
                              skip_group_check=True)

            def shift_scores(n):
                c0, c1 = T_CHUNKS[n]
                for c in range(c0, c1):
                    m, at = chunk_rows(c)
                    last = pe.matmul(bank[3 + n][0:m, (c - c0) * P:(c - c0) * P + P], headsel[:, at:at + m],
                                     shift_t[:, :], start=False, stop=(c == c1 - 1), skip_group_check=True)
                last.then_inc(score_mm, 1)

            def attn_transpose(b):
                pe.wait_ge(attn_done, b + 1)
                if not (isinstance(b, int) and b == 0):
                    pe.wait_ge(lg_done, b)
                pe.transpose(M0[:, 0:P], attn[:, :], ident[:, :]).then_inc(at_mm, 1)

            def project_out(b):
                pe.wait_ge(at_done, b + 1)
                pe.matmul(M0[:, 0:D], attn_t[:, :], wo_g[:, :], start=True, stop=True).then_inc(wo_mm, 1)

            def norm_transpose(b, k):
                pe.wait_ge(xn2_done, b + 1)
                pe.transpose(M0[:, 0:P], rows[:, k % 2, D:2 * D], ident[:, :]).then_inc(x2t_mm, 1)

            def router(b):
                pe.wait_ge(x2t_done, b + 1)
                pe.matmul(M0[:, 0:E], xn2_t[:, :], sw_sb[:, :], start=True, stop=True).then_inc(lg_mm, 1)

            def weigh_values(b, k):
                for c in range(CH):
                    if c % 4 == 0:
                        pe.wait_ge(exp_done, b * T_BANKS + c // 4 + 1)
                    m, _ = chunk_rows(c)
                    last = pe.matmul(M1[:, W0[c] * HV:(W0[c] + W) * HV], probs[0:m, c * P:c * P + P],
                                     v_bd[0:m, c * W:(c + 1) * W, bass.ds(b, 1), :].rearrange("p h b d -> p h (b d)"),
                                     start=(c == 0), stop=(c == CH - 1), skip_group_check=True)
                last.then_inc(pv_mm, 1)

            def attention(b, k):
                scores(b, k, 0)
                if k >= 2:
                    norm_transpose(b - 2, k - 2)
                scores(b, k, 1)
                if k >= 2:
                    router(b - 2)
                pe.wait_ge(shift_done, b + 1)
                if k >= 1:
                    pe.wait_ge(attn_done, b)
                pe.transpose(M1.bitcast(BF16)[:, 0:P], shift[:, k % 2, :], identb[:, :]).then_inc(shiftt_mm, 1)
                scores(b, k, 2)
                if k >= 1:
                    attn_transpose(b - 1)
                pe.wait_ge(shiftt_done, b + 1)
                for n in range(T_BANKS):
                    shift_scores(n)
                if k >= 1:
                    project_out(b - 1)
                if k + 1 < B:
                    energies(b + 1, k + 1)
                weigh_values(b, k)

            pe.wait_ge(k_done, G)
            pe.wait_ge(v_done, G)
            pe.wait_ge(vtail_done, G)
            pe.wait_ge(v_ones, 6)
            pe.wait_ge(q_done, G)
            pe.wait_ge(qb_done, G)
            pe.wait_ge(sel_done, 3)
            pe.wait_ge(identb_done, 1)
            pe.wait_ge(ld_router, 32)
            energies(0, 0)
            for_seqs(pe, attention)
            norm_transpose(B - 2, B - 2)
            router(B - 2)
            attn_transpose(B - 1)
            project_out(B - 1)
            norm_transpose(B - 1, B - 1)
            router(B - 1)

            pe.wait_ge(oh_done, 1)
            pe.wait_ge(const_done, 14)
            pe.matmul(bank[0][:, 0:B * E], before[:, :], onehotb[:, :, :].rearrange("p b e -> p (b e)"),
                      start=True, stop=False, skip_group_check=True)
            for b in range(B):
                last = pe.matmul(bank[0][:, (b + 1) * E:(B + 1) * E].rearrange("p (n e) -> p n e", e=E), ones[:, :],
                                 onehotb[:, b:b + 1, :].broadcast_to([P, B - b, E]),
                                 start=False, stop=(b == B - 1), skip_group_check=True)
            last.then_inc(rank_mm, 1)
            pe.wait_ge(tileval_done, 2)
            for b in range(B):
                pe.wait_ge(rowhot_done, b + 1)
                last = pe.matmul(bank[1][:, 0:2 * TILES], row_hot[:, b, :],
                                 tile_val[:, b, :, :].rearrange("p s t -> p (s t)"), start=(b == 0), stop=(b == B - 1))
            last.then_inc(tok_mm, 1)
            pe.wait_ge(ld_w2, 16)
            pe.wait_ge(expert_done, 1)

            def rows_transpose(t, k):
                slot = k % GATHER_RING
                pe.wait_ge(gathered[slot], fill_count(t, k, GATHER_RING))
                if k >= 2:
                    pe.wait_ge(xgt_done, t - 1)
                pe.transpose(bank[k % 2][:, 0:P], gat[slot][:, D:2 * D], ident[:, :]).then_inc(xgt_mm, 1)

            def up(t, k):
                pe.wait_ge(xgt_done, t + 1)
                pe.wait_ge(w1_ready[k % RING], fill_count(t, k, RING))
                if k >= 2:
                    pe.wait_ge(hid_done, t - 1)
                for c in range(FC):
                    last = pe.matmul(bank[2 + k % 2][:, c * P:c * P + P], w1_ring[:, k % RING, c * P:c * P + P],
                                     xg_t[:, k % 2, :], start=(c == 0), stop=(c == FC - 1), skip_group_check=True)
                last.then_inc(up_mm, 1)

            def down(t, k):
                e = pe.value_load(expert[0:1, bass.ds(t, 1)], min_val=0, max_val=E - 1)
                pe.wait_ge(hid_done, t + 1)
                if k >= 2:
                    pe.wait_ge(yb_done, t - 1)
                for c in range(FC):
                    last = pe.matmul(bank[4 + k % 2][:, 0:D], hid[:, k % 2, c, :],
                                     w2_sb[:, bass.ds(e, 1), c, :].rearrange("p a d -> p (a d)"),
                                     start=(c == 0), stop=(c == FC - 1))
                last.then_inc(down_mm, 1)

            def ffn(t, k):
                rows_transpose(t, k)
                if k >= 1:
                    up(t - 1, k - 1)
                if k >= 2:
                    down(t - 2, k - 2)

            for_tiles(pe, ffn)
            up(TILES - 1, TILES - 1)
            down(TILES - 2, TILES - 2)
            down(TILES - 1, TILES - 1)

        @block.vector
        def _(dve):
            dve.memset(v_flat[:, 0:ZERO_SPLIT[0]], 0.0).then_inc(vbd_zero, 1)
            dve.wait_ge(wrep_mm, 1)
            dve.tensor_copy(wrep[:, :, :], bank[7][:, 0:3 * HV].rearrange("p (n d) -> p n d", n=3)).then_inc(wrep_done, 1)
            dve.wait_ge(wrep_done, 1)
            dve.wait_ge(const_done, 3)
            for n in range(3):
                last = dve.tensor_tensor(wbd[:, n, :, :], wrep[:, n:n + 1, 0:HD].broadcast_to([P, H, HD]),
                                         headmask[:, :].rearrange("p (h a) -> p h a", a=1).broadcast_to([P, H, HD]),
                                         ALU.mult)
            last.then_inc(wbd_done, 1)
            dve.tensor_copy(bv_cols[:, :], wrep[:, 1, HD:HV].broadcast_to([P, P])).then_inc(bvc_done, 1)
            for g in range(G):
                dve.wait_ge(ctxt_done, g + 1)
                keys = bank[g][:, 0:J * L].rearrange("p (j a l) -> p j a l", j=J, a=1)
                dve.tensor_copy(ctx_t[:, g * J:g * J + J, P:P + TAIL_ROWS].rearrange("p j (a l) -> p j a l", a=TAIL_HEADS),
                                keys[:, :, :, HEAD_ROWS:L].broadcast_to([P, J, TAIL_HEADS, TAIL_KEYS])).then_inc(ctxtail_done, 1)
                dve.wait_ge(ld_x[g], 16)
                for b in range(g * J, g * J + J):
                    dve.bn_stats(stats1[:, b, :], x_sb[:, b, :]).then_inc(st1_done, 1)
                for b in range(g * J, g * J + J):
                    dve.wait_ge(st1_done, b + 1)
                    dve.bn_aggr(mv1[:, b, :], stats1[:, b, :]).then_inc(mv1_done, 1)
            dve.wait_ge(mv1_done, B)
            dve.tensor_scalar(half_var1[:, :], mv1[:, :, 1], EPS, 0.5, ALU.add, ALU.mult).then_inc(rstd1_step, 1)
            dve.wait_ge(rstd1_step, 1)
            dve.wait_ge(guess1_done, 1)
            for n, (y, better) in enumerate(((guess1, rstd1), (rstd1, rstd1))):
                dve.tensor_tensor(newton1[:, :], y[:, :], half_var1[:, :], ALU.mult).then_inc(rstd1_step, 1)
                dve.wait_ge(rstd1_step, 3 * n + 2)
                dve.tensor_tensor(newton1[:, :], newton1[:, :], y[:, :], ALU.mult).then_inc(rstd1_step, 1)
                dve.wait_ge(rstd1_step, 3 * n + 3)
                dve.scalar_tensor_tensor(better[:, :], newton1[:, :], 1.5, y[:, :], ALU.subtract, ALU.mult,
                                         reverse0=True).then_inc(rstd1_step, 1)
                dve.wait_ge(rstd1_step, 3 * n + 4)
            for g in range(G):
                js = slice(g * J, g * J + J)
                for j in range(J):
                    b = g * J + j
                    dve.tensor_scalar(xn1[:, b, :], x_sb[:, b, :], mv1[:, b, 0:1], rstd1[:, b:b + 1],
                                      ALU.subtract, ALU.mult).then_inc(xn1_done, 1)
                if g == 0:
                    dve.wait_ge(obias_mm, 1)
                    dve.scalar_tensor_tensor(out_bias[:, :], bo_bc[:, :], tanhs[:, 0:1], bank[7][:, 0:D],
                                             ALU.mult, ALU.add).then_inc(obias_done, 1)
                    dve.tensor_tensor(sel[:, :], ident[:, 0:H], ident[:, H:2 * H], ALU.add).then_inc(sel_done, 1)
                    dve.wait_ge(sel_done, 1)
                    at = 0
                    for keys in (HEAD_ROWS, TAIL_KEYS):
                        dve.tensor_copy(headsel[:, at:at + H * keys].rearrange("p (h l) -> p h l", h=H),
                                        sel[:, :].rearrange("p (h a) -> p h a", a=1).broadcast_to([P, H, keys])
                                        ).then_inc(sel_done, 1)
                        at += H * keys
                    dve.tensor_copy(identb[:, :], ident[:, :]).then_inc(identb_done, 1)
                dve.wait_ge(vtail_mm, g + 1)
                dve.wait_ge(vbd_zero, 1 + len(ZERO_SPLIT))
                dve.wait_ge(const_done, 4)
                for n in range(2):
                    h0 = (CA + n) * W + n * TAIL_HEADS - W0[CA + n]
                    last = dve.tensor_tensor(
                        v_bd[0:TAIL_ROWS, h0:h0 + TAIL_HEADS, js, 0:HD].rearrange("l h j d -> l j h d"),
                        bank[4 + g % 2][0:TAIL_ROWS, :].rearrange("l (j n h d) -> l j n h d", j=J, n=2, d=HD)[:, :, n, :, :],
                        tailmask[0:TAIL_ROWS, :].rearrange("p (a h b) -> p a h b", a=1, b=1)
                        .broadcast_to([TAIL_ROWS, J, TAIL_HEADS, HD]), ALU.mult)
                last.then_inc(vtail_done, 1)

            def row_max(b, k):
                dve.wait_ge(energy_mm, b + 1)
                full = [n for n, (h0, h1) in enumerate(E_HEADS) if h1 - h0 == PER_BANK]
                dve.tensor_reduce(emax[:, k % 2, 0:len(full) * PER_BANK].rearrange("p (n h) -> p n h", n=len(full)),
                                  ps_e[:, 0:len(full), 0:PER_BANK * L].rearrange("p n (h l) -> p n h l", l=L),
                                  AX, ALU.max)
                h0, h1 = E_HEADS[-1]
                dve.tensor_reduce(emax[:, k % 2, h0:h1], ps_e[:, E_BANKS - 1, 0:(h1 - h0) * L]
                                  .rearrange("p (h l) -> p h l", l=L), AX, ALU.max).then_inc(emax_done, 1)
                dve.wait_ge(emax_done, b + 1)
                if k >= 2:
                    dve.wait_ge(shiftt_mm, b - 1)
                dve.tensor_scalar(shift[:, k % 2, 0:H], emax[:, k % 2, :], -1.0, None, ALU.mult).then_inc(shift1_done, 1)
                dve.wait_ge(shift1_done, b + 1)
                dve.scalar_tensor_tensor(shift[:, k % 2, H:2 * H], emax[:, k % 2, :], -1.0, shift[:, k % 2, 0:H],
                                         ALU.mult, ALU.subtract).then_inc(shift_done, 1)

            def normalise(b):
                dve.wait_ge(pv_mm, b + 1)
                o = M1[:, 0:H * HV].rearrange("p (h d) -> p h d", h=H)
                dve.reciprocal(rden[:, :], o[:, :, HD]).then_inc(rden_done, 1)
                dve.wait_ge(rden_done, b + 1)
                if not (isinstance(b, int) and b == 0):
                    dve.wait_ge(at_mm, b)
                dve.tensor_tensor(attn[:, :].rearrange("p (h d) -> p h d", h=H), o[:, :, 0:HD],
                                  rden[:, :].rearrange("p (h a) -> p h a", a=1).broadcast_to([P, H, HD]),
                                  ALU.mult).then_inc(attn_done, 1)

            def residual_norm(b, k, row_wait):
                dve.wait_ge(wo_mm, b + 1)
                if isinstance(b, int) and b in (0, J, 2 * J, 3 * J):
                    dve.wait_ge(xres_done, b // J + 1)
                if k == 2:
                    dve.wait_ge(xres_done, G)
                if k >= 2:
                    dve.wait_ge(x2t_mm, b - 1)
                if row_wait is not None:
                    dve.wait_ge(row_store[k % 2], row_wait)
                x1 = rows[:, k % 2, 0:D]
                dve.tensor_tensor(x1, M0[:, 0:D], x_sb[:, bass.ds(b, 1), :].rearrange("p a d -> p (a d)"),
                                  ALU.add).then_inc(x1_done, 1)
                dve.wait_ge(x1_done, b + 1)
                dve.bn_stats(stats2[:, :], x1).then_inc(st2_done, 1)
                dve.wait_ge(st2_done, b + 1)
                detach(dve)
                dve.bn_aggr(mv2[:, :], stats2[:, :]).then_inc(mv2_done, 1)
                dve.wait_ge(mv2_done, b + 1)
                dve.tensor_scalar(half_var2[:, :], mv2[:, 1:2], EPS, 0.5, ALU.add, ALU.mult).then_inc(hv2_done, 1)

            def norm(b, k):
                dve.wait_ge(guess2_done, b + 1)
                for n, y in enumerate((guess2, rstd2)):
                    dve.tensor_scalar(newton2[:, :], y[:, :], y[:, :], half_var2[:, :],
                                      ALU.mult, ALU.mult).then_inc(rstd2_step, 1)
                    dve.wait_ge(rstd2_step, b * 4 + (2 * n + 1))
                    dve.scalar_tensor_tensor(rstd2[:, :], newton2[:, :], 1.5, y[:, :], ALU.subtract, ALU.mult,
                                             reverse0=True).then_inc(rstd2_step, 1)
                    dve.wait_ge(rstd2_step, b * 4 + (2 * n + 2))
                dve.tensor_scalar(rows[:, k % 2, D:2 * D], rows[:, k % 2, 0:D], mv2[:, 0:1], rstd2[:, 0:1],
                                  ALU.subtract, ALU.mult).then_inc(xn2_done, 1)

            def router_bias(b):
                dve.wait_ge(lg_mm, b + 1)
                dve.tensor_tensor(logits[:, bass.ds(b, 1), :].rearrange("p a e -> p (a e)"), M0[:, 0:E], sbias[:, :],
                                  ALU.add).then_inc(lg_done, 1)

            def attention(b, k):
                if k >= 1:
                    normalise(b - 1)
                if k >= 2:
                    router_bias(b - 2)
                dve.wait_ge(shiftt_mm, b + 1)
                if k >= 1:
                    dve.wait_ge(score_mm, b * T_BANKS)
                dve.tensor_copy(shift_t[:, :], M1.bitcast(BF16)[:, 0:P]).then_inc(shiftt_done, 1)
                if k >= 1:
                    wait = None
                    if k >= 3:
                        wait = (b - 1 - (k - 1) % 2) * 8
                    residual_norm(b - 1, k - 1, wait)
                if k + 1 < B:
                    row_max(b + 1, k + 1)
                if k >= 1:
                    norm(b - 1, k - 1)

            dve.wait_ge(pad_zero, 1)
            dve.wait_ge(ld_router, 32)
            row_max(0, 0)
            for_seqs(dve, attention)
            normalise(B - 1)
            router_bias(B - 2)
            residual_norm(B - 1, B - 1, (B - 1 - (B - 1) % 2) * 8)
            norm(B - 1, B - 1)
            router_bias(B - 1)

            done = [0]

            def step(ins):
                ins.then_inc(cs, 1)
                done[0] += 1
                dve.wait_ge(cs, done[0])

            def over_e(ap):
                return ap.rearrange("p (b a) -> p b a", a=1).broadcast_to([P, B, E])

            dve.wait_ge(lg_done, B)
            dve.wait_ge(const_done, 14)
            step(dve.tensor_reduce(lmax[:, :], logits[:, :, :], AX, ALU.max))
            dve.tensor_tensor(lsub[:, :, :], logits[:, :, :], over_e(lmax[:, :]), ALU.subtract).then_inc(lsub_done, 1)
            dve.wait_ge(lsub_done, 1)
            step(dve.scalar_tensor_tensor(is_max[:, :, :], lsub[:, :, :], 0.0,
                                          prefer_low[:, :].rearrange("p (a e) -> p a e", a=1).broadcast_to([P, B, E]),
                                          ALU.is_equal, ALU.mult))
            step(dve.tensor_reduce(pick[:, :], is_max[:, :, :], AX, ALU.max))
            dve.tensor_tensor(onehotb[:, :, :], is_max[:, :, :], over_e(pick[:, :]), ALU.is_equal).then_inc(oh_done, 1)
            dve.wait_ge(lexp_done, 1)
            step(dve.tensor_reduce(lsum[:, :], lexp[:, :, :], AX, ALU.add))
            step(dve.reciprocal(lsum[:, :], lsum[:, :]))
            dve.tensor_scalar(scale_tok[:, :], lsum[:, :], tanhs[:, 1:2], None, ALU.mult).then_inc(scale_done, 1)
            dve.wait_ge(rank_mm, 1)
            count = bank[0][:, B * E:(B + 1) * E]
            step(dve.tensor_tensor(over[:, :, :], count.rearrange("p (e a) -> p e a", a=1).broadcast_to([P, E, B]),
                                   rank_step[:, :].rearrange("p (a b) -> p a b", a=1).broadcast_to([P, E, B]),
                                   ALU.is_gt))
            step(dve.tensor_reduce(n_tiles[:, :], over[:, :, :], AX, ALU.add))
            step(dve.tensor_tensor(base_prod[:, :, :], e_before[:, :, :],
                                   n_tiles[:, :].rearrange("p (a e) -> p a e", a=1).broadcast_to([P, E, E]), ALU.mult))
            dve.tensor_reduce(base[:, :], base_prod[:, :, :], AX, ALU.add).then_inc(base_done, 1)
            dve.wait_ge(base_done, 1)
            step(dve.scalar_tensor_tensor(slot_e[:, :, :], base[:, :].rearrange("p (a e) -> p a e", a=1).broadcast_to([P, B, E]),
                                          float(P), bank[0][:, 0:B * E].rearrange("p (b e) -> p b e", e=E),
                                          ALU.mult, ALU.add))
            step(dve.tensor_tensor(slot_m[:, :, :], slot_e[:, :, :], onehotb[:, :, :], ALU.mult))
            step(dve.tensor_reduce(slot[:, :], slot_m[:, :, :], AX, ALU.add))
            step(dve.tensor_copy(slot_int[:, :], slot[:, :]))
            step(dve.tensor_scalar(slot_low[:, :], slot_int[:, :], P - 1, None, ALU.bitwise_and))
            step(dve.tensor_copy(slot_row[:, :], slot_low[:, :]))
            step(dve.tensor_tensor(slot_start[:, :], slot[:, :], slot_row[:, :], ALU.subtract))
            step(dve.tensor_tensor(tile_hot[:, :, :],
                                   tile_start[:, :].rearrange("p (a t) -> p a t", a=1).broadcast_to([P, B, TILES]),
                                   slot_start[:, :].rearrange("p (b a) -> p b a", a=1).broadcast_to([P, B, TILES]),
                                   ALU.is_equal))
            dve.tensor_scalar(tile_val[:, :, 0, :], tile_hot[:, :, :], iota_part[:, 0:1], None,
                              ALU.mult).then_inc(tileval_done, 1)
            dve.tensor_tensor(tile_val[:, :, 1, :], tile_hot[:, :, :],
                              seq_code[:, :].rearrange("p (b a) -> p b a", a=1).broadcast_to([P, B, TILES]),
                              ALU.mult).then_inc(tileval_done, 1)
            for b in range(B):
                dve.tensor_scalar(row_hot[:, b, :], iota_row[:, :], slot_row[:, b:b + 1], None,
                                  ALU.is_equal).then_inc(rowhot_done, 1)
            dve.wait_ge(tok_mm, 1)
            step(dve.tensor_scalar(tok_a[:, :], bank[1][:, TILES:2 * TILES], -float(P), float(NTOK), ALU.mult, ALU.add))
            dve.tensor_tensor(tok[:, :], tok_a[:, :], bank[1][:, 0:TILES], ALU.add).then_inc(tok_done, 1)

            step(dve.tensor_tensor(end[:, :], base[0:1, :], n_tiles[0:1, :], ALU.add))
            step(dve.tensor_tensor(past[:, :, :], tile_no[:, :].rearrange("p (t a) -> p t a", a=1).broadcast_to([1, TILES, E]),
                                   end[:, :].rearrange("p (a e) -> p a e", a=1).broadcast_to([1, TILES, E]), ALU.is_ge))
            step(dve.tensor_reduce(expert_f[:, :], past[:, :, :], AX, ALU.add))
            dve.tensor_scalar(expert[:, :], expert_f[:, :], float(E - 1), None, ALU.min).then_inc(expert_done, 1)

            dve.wait_ge(ld_b2, 16)

            def rows_copy(t, k):
                dve.wait_ge(xgt_mm, t + 1)
                if k >= 2:
                    dve.wait_ge(up_mm, t - 1)
                dve.tensor_copy(xg_t[:, k % 2, :], bank[k % 2][:, 0:P]).then_inc(xgt_done, 1)

            def combine(t, k, scatter_wait):
                e = dve.value_load(expert[0:1, bass.ds(t, 1)], min_val=0, max_val=E - 1)
                dve.wait_ge(down_mm, t + 1)
                dve.tensor_tensor(yb[:, k % 2, :], bank[4 + k % 2][:, 0:D],
                                  b2_bc[:, bass.ds(e, 1), :].rearrange("p a d -> p (a d)"), ALU.add).then_inc(yb_done, 1)
                dve.wait_ge(yb_done, t + 1)
                if scatter_wait is not None:
                    dve.wait_ge(scattered[k % RING], scatter_wait)
                g = gat[k % GATHER_RING]
                dve.scalar_tensor_tensor(res[k % RING][:, :], yb[:, k % 2, :], g[:, 2 * D:ROW], g[:, 0:D],
                                         ALU.mult, ALU.add).then_inc(res_done, 1)

            def scatters_before(t, k):
                return (t - k % RING) * (16 // RING) if k >= RING else None

            def rows_and_results(t, k):
                rows_copy(t, k)
                if k >= 2:
                    combine(t - 2, k - 2, scatters_before(t - 2, k - 2))

            for_tiles(dve, rows_and_results)
            for t in range(TILES - 2, TILES):
                combine(t, t, scatters_before(t, t))


_HEAD_WEIGHTS = [("L0_xattn_wk", "L0_xattn_bk"), ("L0_xattn_wv", "L0_xattn_bv"), ("L0_xattn_wq", "L0_xattn_bq")]
_AS_THEY_ARE = ["L0_xattn_bo", "L0_ffn_switch_w", "L0_ffn_switch_b", "L0_ffn_w1"]


def kernel(**inputs):
    import numpy as np
    import concourse.bacc as bacc
    from concourse.bass_utils import run_bass_kernel_spmd

    given = {name: np.asarray(a) for name, a in inputs.items()}
    laid = {name: given[name] for name in ("x", "ctx_1024", "g_xattn", "g_ffn")}
    laid["w_heads"] = np.stack([np.concatenate([given[w].T, given[b][:, None]], axis=1) for w, b in _HEAD_WEIGHTS], axis=1)
    laid["wo_t"] = given["L0_xattn_wo"].T
    laid |= {name: given[name] for name in _AS_THEY_ARE}
    laid["b1_t"] = given["L0_ffn_b1"].reshape(-1, P).T
    laid |= {name: given[name] for name in ("L0_ffn_w2", "L0_ffn_b2")}

    nc = bacc.Bacc("TRN2", target_bir_lowering=False, num_devices=1)
    arrays, args = {}, []
    for name, a in laid.items():
        arrays[f"in_{name}"] = np.ascontiguousarray(a)
        args.append(nc.dram_tensor(f"in_{name}", a.shape, mybir.dt.from_np(a.dtype), kind="ExternalInput").ap())
    B, S, D = inputs["x"].shape
    out = nc.dram_tensor("out_rows", (B * S, D), F32, kind="ExternalOutput").ap()
    table = nc.dram_tensor("row_table", (B * S, 2 * D + 1), F32).ap()
    flamingo_layer(nc, *args, out, table)
    r = run_bass_kernel_spmd(nc, [arrays], core_ids=[0])
    return r.results[0]["out_rows"].reshape(B, S, D)
```

```python
import math
from contextlib import ExitStack

import concourse.bass as bass
from concourse import mybir

F32 = mybir.dt.float32
BF16 = mybir.dt.bfloat16
F16 = mybir.dt.float16
I32 = mybir.dt.int32
U32 = mybir.dt.uint32
ALU = mybir.AluOpType
ACT = mybir.ActivationFunctionType
AX = mybir.AxisListType.X

P = 128


def flamingo_layer(nc, x, ctx_in, g_xattn, g_ffn, w_heads, wo_t, bo,
                   switch_w, switch_b, w1, b1_t, w2, b2, out, table):
    B, S, D = x.shape
    L = ctx_in.shape[1]
    HD = w_heads.shape[0]
    H = D // HD
    E, _, F = w1.shape
    FC = F // P
    assert S == P and D == P and B == 16
    J = 4
    G = B // J
    NTOK = B * S
    assert NTOK <= 2048, "a token's code is exact in fp16"
    TILES = NTOK // P + E - 1
    RING = 4
    GATHER_RING = 8
    PEEL = 7
    assert (TILES - PEEL) % GATHER_RING == 0 and GATHER_RING % RING == 0
    HL = H * L
    HV = HD + 1
    HEAD_ROWS = P // 2
    TAIL_KEYS = L - HEAD_ROWS
    TAIL_HEADS = H // 2
    TAIL_ROWS = TAIL_HEADS * TAIL_KEYS
    CA = H // 2
    CH = CA + H // TAIL_HEADS
    assert 0 < TAIL_ROWS <= P
    W = 11
    assert W * HV >= 96
    W0 = [min(2 * c, H - W) for c in range(CA)] + [0, H - W]
    N0 = (H - W) // 2 + 1
    SCALE = float(D) ** -0.5
    EPS = 1e-5
    GUESS_SCALE = -0.5 * math.log(2.0) / 2 ** 23
    GUESS_BIAS = 0.5 * math.log(2.0) * (126 - 0.043)
    ROW = 2 * D + 1
    PER_BANK = 512 // L
    E_HEADS = [(h, min(h + PER_BANK, H)) for h in range(0, H, PER_BANK)]
    E_BANKS = len(E_HEADS)
    T_CHUNKS = [(0, 4), (4, 8), (8, CH)]
    T_BANKS = len(T_CHUNKS)
    assert E_BANKS + T_BANKS == 6 and CA == 8
    OWN = [(slice(0, N0), slice(0, N0 * W, W)),
           (slice(N0, CA), slice(N0 * W + 2 * N0 - (H - W), (CA - 1) * W + 2 * (CA - 1) - (H - W) + 1, W + 2))]

    with ExitStack() as ctx:
        def sb(name, shape, dt=F32):
            return ctx.enter_context(nc.sbuf_tensor(name, shape, dt))

        def sem(name):
            return ctx.enter_context(nc.semaphore(name))

        ident = sb("ident", [P, P])
        identb = sb("identb", [P, P], BF16)
        rep = sb("rep", [HD, P])
        headmask = sb("headmask", [P, H])
        headsel = sb("headsel", [P, HL], BF16)
        sel = sb("sel", [P, H])
        tailmask = sb("tailmask", [P, TAIL_HEADS])
        busy_src = sb("busy_src", [P, 512], BF16)
        zero_col, guess_bias = sb("zero_col", [P, 1]), sb("guess_bias", [P, 1])
        before = sb("before", [P, P], BF16)
        ones = sb("ones", [P, P], BF16)
        iota_row = sb("iota_row", [P, P], BF16)
        tile_start = sb("tile_start", [P, TILES], BF16)
        tile_no = sb("tile_no", [1, TILES])
        rank_step = sb("rank_step", [P, B])
        prefer_low = sb("prefer_low", [P, E])
        token_code = sb("token_code", [P, B], F16)
        e_before = sb("e_before", [P, E, E])
        gates = sb("gates", [P, 2])
        tanhs = sb("tanhs", [P, 2])
        w_small = sb("w_small", [HD, 3, HV])
        wrep = sb("wrep", [P, 3, HV])
        wbd = sb("wbd", [P, 3, H, HD])
        bv_cols = sb("bv_cols", [P, P])
        wo_sb = sb("wo_sb", [P, D])
        wo_g = sb("wo_g", [P, D])
        bo_bc = sb("bo_bc", [P, D])
        out_bias = sb("out_bias", [P, D])
        sw_sb = sb("sw_sb", [P, E])
        sbias = sb("sbias", [P, E])
        w2_sb = sb("w2_sb", [P, E, FC, D])
        b1_sb = sb("b1_sb", [P, E, FC])
        b2_bc = sb("b2_bc", [P, E, D])
        ctx_sb = sb("ctx_sb", [L, B, D])
        ctx_t = sb("ctx_t", [P, B, P + TAIL_ROWS])
        k_t = sb("k_t", [P, B, L])
        x_sb = sb("x_sb", [P, B, D])
        stats1 = sb("stats1", [P, B, 6])
        mv1 = sb("mv1", [P, B, 2])
        guess1, half_var1, newton1, rstd1 = (
            sb(n, [P, B]) for n in ("guess1", "half_var1", "newton1", "rstd1"))
        guess2, half_var2, newton2 = (sb(n, [P, 1]) for n in ("guess2", "half_var2", "newton2"))
        w1_ring = sb("w1_ring", [P, RING, F])
        xn1 = w1_ring[:, :, :].rearrange("p r f -> p (r f)").rearrange("p (b d) -> p b d", b=B)
        xn1_t = sb("xn1_t", [P, 2, J, P])
        q_t = sb("q_t", [P, B, P])
        q_tb = sb("q_tb", [P, B, P], BF16)
        v_bd = sb("v_bd", [P, CH * W, B, HV])
        k_bd = sb("k_bd", [P, 2, HL])
        k_bdb = sb("k_bdb", [P, 2, HL], BF16)
        emax = sb("emax", [P, 2, H])
        shift = sb("shift", [P, 2, P], BF16)
        shift_t = sb("shift_t", [P, P], BF16)
        probs = sb("probs", [P, CH * P])
        rden = sb("rden", [P, H])
        attn = sb("attn", [P, D])
        attn_t = sb("attn_t", [P, P])
        stats2 = sb("stats2", [P, 6])
        mv2 = sb("mv2", [P, 2])
        rstd2 = sb("rstd2", [P, 1])
        rows = sb("rows", [P, 2, 2 * D])
        xn2_t = sb("xn2_t", [P, P])
        logits = sb("logits", [P, B, E])
        gelu_warm = sb("gelu_warm", [P, 1])
        lmax = sb("lmax", [P, B])
        lsub = sb("lsub", [P, B, E])
        lexp = sb("lexp", [P, B, E])
        lsum = sb("lsum", [P, B])
        scale_tok = sb("scale_tok", [P, B])
        is_max = sb("is_max", [P, B, E])
        pick = sb("pick", [P, B])
        onehotb = sb("onehotb", [P, B, E], BF16)
        over = sb("over", [P, E, B])
        n_tiles = sb("n_tiles", [P, E])
        base_prod = sb("base_prod", [P, E, E])
        base = sb("base", [P, E])
        end = sb("end", [1, E])
        slot_e = sb("slot_e", [P, B, E])
        slot_m = sb("slot_m", [P, B, E])
        slot = sb("slot", [P, B])
        slot_int = sb("slot_int", [P, B], I32)
        slot_low = sb("slot_low", [P, B], I32)
        slot_row = sb("slot_row", [P, B])
        slot_start = sb("slot_start", [P, B], BF16)
        row_hot = sb("row_hot", [P, B, P], F16)
        tile_code = sb("tile_code", [P, B, TILES], F16)
        tile_hot = sb("tile_hot", [P, B, TILES], F16)
        past = sb("past", [1, TILES, E])
        expert_f = sb("expert_f", [1, TILES])
        expert = sb("expert", [1, TILES], I32)
        tok = sb("tok", [P, TILES], U32)
        hid = sb("hid", [P, 2, FC, P])
        gat = [ctx_t[:, :, :].rearrange("p b l -> p (b l)")[:, i * ROW:(i + 1) * ROW] for i in range(GATHER_RING)]
        xg_t = sb("xg_t", [P, 2, P])
        yb = sb("yb", [P, 2, D])
        res = [sb(f"res{i}", [P, D]) for i in range(RING)]

        pe_bank = [ctx.enter_context(nc.psum_tensor(f"ps{i}", [P, 512], F32)) for i in range(2)]
        ps_e = ctx.enter_context(nc.psum_tensor("ps_e", [P, E_BANKS, 512], F32))
        ps_t = ctx.enter_context(nc.psum_tensor("ps_t", [P, T_BANKS, 512], F32))
        bank = [ps_e[:, i, :] for i in range(E_BANKS)] + [ps_t[:, i, :] for i in range(T_BANKS)] \
            + [pe_bank[0][:, :], pe_bank[1][:, :]]
        M0, M1 = bank[6], bank[7]
        XT_BANK = [bank[i] for i in (6, 6, 4, 5)]
        Q_BANK = [bank[i] for i in (7, 7, 7, 6)]
        assert G == 4

        ld_small, ld_misc = sem("ld_small"), sem("ld_misc")
        ld_ctx, ld_x = [sem(f"ld_ctx{g}") for g in range(G)], [sem(f"ld_x{g}") for g in range(G)]
        ld_router, ld_w2, ld_b1, ld_b2 = sem("ld_router"), sem("ld_w2"), sem("ld_b1"), sem("ld_b2")
        passed = sem("passed")
        zeroed = sem("zeroed")
        const_done, identb_done = sem("const_done"), sem("identb_done")
        mask_step = sem("mask_step")
        vbd_zero = sem("vbd_zero")
        cols_ready, busy_ready = sem("cols_ready"), sem("busy_ready")
        sel_done = sem("sel_done")
        v_ones = sem("v_ones")
        pad_zero = sem("pad_zero")
        wrep_mm = sem("wrep_mm")
        wrep_done = sem("wrep_done")
        wbd_done = sem("wbd_done")
        tanh_done = sem("tanh_done")
        wog_done = sem("wog_done")
        bvc_done = sem("bvc_done")
        obias_mm = sem("obias_mm")
        obias_done = sem("obias_done")
        xres_done = sem("xres_done")
        ctxt_mm, ctxt_done, ctxtail_done = sem("ctxt_mm"), sem("ctxt_done"), sem("ctxtail_done")
        k_mm, k_done = sem("k_mm"), sem("k_done")
        v_mm, vtail_mm, v_done, vtail_done = sem("v_mm"), sem("vtail_mm"), sem("v_done"), sem("vtail_done")
        st1_done, mv1_done, rstd1_step, xn1_done = sem("st1_done"), sem("mv1_done"), sem("rstd1_step"), sem("xn1_done")
        guess1_done = sem("guess1_done")
        xt_mm, xt_done = sem("xt_mm"), sem("xt_done")
        q_mm, q_done, qb_done = sem("q_mm"), sem("q_done"), sem("qb_done")
        keys_ready, keysb_ready, keysb_first = sem("keys_ready"), sem("keysb_ready"), sem("keysb_first")
        energy_mm, emax_done, shift1_done, shift_done = sem("energy_mm"), sem("emax_done"), sem("shift1_done"), sem("shift_done")
        shiftt_mm, shiftt_done = sem("shiftt_mm"), sem("shiftt_done")
        score_mm, exp_done = sem("score_mm"), sem("exp_done")
        pv_mm, rden_done, attn_done = sem("pv_mm"), sem("rden_done"), sem("attn_done")
        at_mm, at_done = sem("at_mm"), sem("at_done")
        wo_mm, x1_done, st2_done, mv2_done, hv2_done, rstd2_step, xn2_done = (
            sem("wo_mm"), sem("x1_done"), sem("st2_done"), sem("mv2_done"), sem("hv2_done"), sem("rstd2_step"), sem("xn2_done"))
        guess2_done = sem("guess2_done")
        x2t_mm, x2t_done, lg_mm, lg_done = sem("x2t_mm"), sem("x2t_done"), sem("lg_mm"), sem("lg_done")
        row_store = [sem("row_store0"), sem("row_store1")]
        route_step = sem("route_step")
        lsub_done, lexp_done, scale_done, scale_store = sem("lsub_done"), sem("lexp_done"), sem("scale_done"), sem("scale_store")
        oh_done, rank_mm, rowhot_done, tilehot_done, tilecode_done, tok_mm = (
            sem("oh_done"), sem("rank_mm"), sem("rowhot_done"), sem("tilehot_done"), sem("tilecode_done"), sem("tok_mm"))
        base_done, expert_step, slotrow_done = sem("base_done"), sem("expert_step"), sem("slotrow_done")
        tok_done, expert_done = sem("tok_done"), sem("expert_done")
        gat_zero = sem("gat_zero")
        gathered = [sem(f"gathered{i}") for i in range(GATHER_RING)]
        w1_ready = [sem(f"w1_ready{i}") for i in range(RING)]
        xgt_mm, xgt_done = sem("xgt_mm"), sem("xgt_done")
        up_mm, hid_done, down_mm = sem("up_mm"), sem("hid_done"), sem("down_mm")
        yb_done, res_done = sem("yb_done"), sem("res_done")
        scattered = [sem(f"scattered{i}") for i in range(RING)]

        block = ctx.enter_context(nc.Block())

        def for_tiles(eng, tile_step):
            for t in range(PEEL):
                tile_step(t, t)
            with eng.Fori(0, (TILES - PEEL) // GATHER_RING) as i:
                for k in range(PEEL, PEEL + GATHER_RING):
                    tile_step(i * GATHER_RING + k, k)

        def for_seqs(eng, seq_step):
            for b in range(3):
                seq_step(b, b)
            with eng.Fori(0, (B - 6) // 2) as i:
                seq_step(i * 2 + 3, 3)
                seq_step(i * 2 + 4, 4)
            for b in range(B - 3, B):
                seq_step(b, b)

        def detach(eng):
            eng.sem_inc(passed, 1)

        def chunk_rows(c):
            return (P, c * P) if c < CA else (TAIL_ROWS, CA * P + (c - CA) * TAIL_ROWS)

        def add_out_bias(pool, g):
            js = slice(g * J, g * J + J)
            pool.tensor_tensor(x_sb[:, js, :], x_sb[:, js, :],
                               out_bias[:, :].rearrange("p (a d) -> p a d", a=1).broadcast_to([P, J, D]),
                               ALU.add).then_inc(xres_done, 1)

        v_flat = v_bd[:, :, :, :].rearrange("p h b d -> p (h b d)")
        ZERO_SPLIT = (3000, 4500, 5400, 6300, 7200)

        KEY_PARTS = ((slice(0, CA * P), slice(0, HEAD_ROWS)), (slice(CA * P, HL), slice(HEAD_ROWS, L)))

        def round_keys(act, b, k):
            act.wait_ge(keys_ready, b + 1)
            for part, keys in KEY_PARTS:
                last = act.activation(k_bdb[:, k % 2, :].rearrange("p (h l) -> p h l", h=H)[:, :, keys],
                                      k_bd[:, k % 2, part].rearrange("p (h l) -> p h l", h=H), ACT.Copy)
            last.then_inc(keysb_ready, 1)

        def build_keys(pool, b, k):
            src = k_t[:, bass.ds(b, 1), :].broadcast_to([P, H, L])
            mask = headmask[:, :].rearrange("p (h a) -> p h a", a=1).broadcast_to([P, H, L])
            for part, keys in KEY_PARTS:
                last = nc.gpsimd.tensor_tensor(k_bd[:, k % 2, part].rearrange("p (h l) -> p h l", h=H), src[:, :, keys],
                                               mask[:, :, keys], ALU.mult)
            last.then_inc(keys_ready, 1)

        def fill_count(t, k, ring):
            if isinstance(t, int):
                return 16 * (t // ring + 1)
            return (t - (k % ring)) * (16 // ring) + 16

        @block.sync
        def _(sp):
            def load_x(g):
                js = slice(g * J, g * J + J)
                sp.dma_start(x_sb[:, js, :], x[js].rearrange("b s d -> s b d")).then_inc(ld_x[g], 16)

            for g in range(G):
                js = slice(g * J, g * J + J)
                sp.dma_start(ctx_sb[:, js, :], ctx_in[js].rearrange("b l d -> l b d")).then_inc(ld_ctx[g], 16)
                if g == 0:
                    sp.dma_start(w_small[:, :, :], w_heads).then_inc(ld_small, 16)
                else:
                    load_x(g - 1)
            load_x(G - 1)
            sp.dma_start(gates[:, 0:1], g_xattn.rearrange("(a b) -> a b", a=1).broadcast_to([P, 1])).then_inc(ld_misc, 16)
            sp.dma_start(gates[:, 1:2], g_ffn.rearrange("(a b) -> a b", a=1).broadcast_to([P, 1])).then_inc(ld_misc, 16)
            sp.dma_start(wo_sb[:, :], wo_t).then_inc(ld_misc, 16)
            sp.dma_start(bo_bc[:, :], bo.rearrange("(a d) -> a d", a=1).broadcast_to([P, D])).then_inc(ld_misc, 16)
            sp.dma_start(sw_sb[:, :], switch_w).then_inc(ld_router, 16)
            sp.dma_start(sbias[:, :], switch_b.rearrange("(a d) -> a d", a=1).broadcast_to([P, E])).then_inc(ld_router, 16)
            sp.dma_start(w2_sb[:, :, :, :], w2.rearrange("e (c p) d -> p e c d", p=P)).then_inc(ld_w2, 16)
            sp.dma_start(b1_sb[:, :, :], b1_t.rearrange("p (e c) -> p e c", e=E)).then_inc(ld_b1, 16)
            sp.dma_start(b2_bc[:, :, :].rearrange("p e d -> p (e d)"),
                         b2.rearrange("(a e) d -> a (e d)", a=1).broadcast_to([P, E * D])).then_inc(ld_b2, 16)

            def store_rows(b, k):
                sp.wait_ge(xn2_done, b + 1)
                sp.dma_start(table[bass.ds(b * P, P), 0:2 * D], rows[:, k % 2, :]).then_inc(row_store[k % 2], 16)

            for_seqs(sp, store_rows)
            sp.wait_ge(scale_done, 1)
            sp.dma_start(table.rearrange("(b p) r -> p b r", p=P)[:, :, 2 * D:ROW],
                         scale_tok[:, :].rearrange("p (b a) -> p b a", a=1),
                         allow_slow_non_contiguous=True).then_inc(scale_store, 16)

            sp.wait_ge(expert_done, 1)

            def load_w1(t, k):
                if k >= RING:
                    sp.wait_ge(up_mm, t - RING + 1)
                e = sp.value_load(expert[0:1, bass.ds(t, 1)], min_val=0, max_val=E - 1)
                sp.dma_start(w1_ring[:, k % RING, :], w1[bass.ds(e, 1)].rearrange("e p f -> p (e f)")
                             ).then_inc(w1_ready[k % RING], 16)

            for_tiles(sp, load_w1)

        @block.gpsimd
        def _(pool):
            pool.memset(zero_col[:, :], 0.0).then_inc(cols_ready, 1)
            pool.memset(guess_bias[:, :], GUESS_BIAS).then_inc(cols_ready, 1)
            pool.memset(rep[:, :], 0.0).then_inc(zeroed, 1)
            pool.memset(ident[:, :], 0.0).then_inc(zeroed, 1)
            pool.memset(headmask[:, :], 1.0).then_inc(zeroed, 1)
            pool.memset(tailmask[:, :], 1.0).then_inc(zeroed, 1)
            pool.wait_ge(zeroed, 4)
            pool.affine_select(ident[:, :], ident[:, :], pattern=[[-1, P]], compare_op=ALU.not_equal,
                               fill=1.0, base=0, channel_multiplier=1).then_inc(const_done, 1)
            pool.affine_select(rep[:, :].rearrange("i (h j) -> i h j", h=H), rep[:, :].rearrange("i (h j) -> i h j", h=H),
                               pattern=[[0, H], [-1, HD]], compare_op=ALU.not_equal,
                               fill=1.0, base=0, channel_multiplier=1).then_inc(const_done, 1)
            for n, (mask, rows_each, heads) in enumerate(((headmask, HD, H), (tailmask, TAIL_KEYS, TAIL_HEADS))):
                pool.affine_select(mask[:, :], mask[:, :], pattern=[[-rows_each, heads]], compare_op=ALU.is_ge,
                                   fill=0.0, base=0, channel_multiplier=1).then_inc(mask_step, 1)
                pool.wait_ge(mask_step, n + 1)
                pool.affine_select(mask[:, :], mask[:, :], pattern=[[rows_each, heads]], compare_op=ALU.is_ge,
                                   fill=0.0, base=rows_each - 1, channel_multiplier=-1).then_inc(const_done, 1)
            pool.memset(v_flat[:, ZERO_SPLIT[-1]:], 0.0).then_inc(vbd_zero, 1)
            pool.memset(shift[:, :, :], 0.0).then_inc(pad_zero, 1)
            pool.wait_ge(vbd_zero, 1 + len(ZERO_SPLIT))
            pool.wait_ge(pad_zero, 1)
            for odd in range(2):
                for n, (_, own) in enumerate(OWN):
                    if odd or n:
                        pool.wait_ge(v_ones, 2 * odd + n)
                    cols = slice(own.start + odd, own.stop + odd, own.step)
                    pool.memset(v_bd[odd * HEAD_ROWS:(odd + 1) * HEAD_ROWS, cols, :, HD:HV], 1.0).then_inc(v_ones, 1)
            for n in range(2):
                pool.wait_ge(v_ones, 4 + n)
                h0 = (CA + n) * W + n * TAIL_HEADS - W0[CA + n]
                pool.tensor_copy(v_bd[0:TAIL_ROWS, h0:h0 + TAIL_HEADS, :, HD],
                                 tailmask[0:TAIL_ROWS, :].rearrange("p (h a) -> p h a", a=1)
                                 .broadcast_to([TAIL_ROWS, TAIL_HEADS, B])).then_inc(v_ones, 1)
            pool.wait_ge(v_ones, 6)
            pool.wait_ge(k_done, 1)
            for b in range(2):
                build_keys(pool, b, b)
            pool.wait_ge(obias_done, 1)
            pool.wait_ge(xn1_done, J)
            add_out_bias(pool, 0)

            def keys_ahead(b, k):
                for g in range(1, G):
                    if k == min(g, 2):
                        pool.wait_ge(xn1_done, (g + 1) * J)
                        add_out_bias(pool, g)
                if k + 2 < B:
                    pool.wait_ge(score_mm, T_BANKS * b + T_BANKS)
                    if k + 2 == J:
                        pool.wait_ge(k_done, G)
                    build_keys(pool, b + 2, k + 2)

            for_seqs(pool, keys_ahead)

            pool.iota(iota_row[:, :], pattern=[[1, P]], base=0, channel_multiplier=0,
                      allow_small_or_imprecise_dtypes=True).then_inc(const_done, 1)
            pool.iota(tile_no[:, :], pattern=[[1, TILES]], base=0, channel_multiplier=0,
                      allow_small_or_imprecise_dtypes=True).then_inc(const_done, 1)
            pool.iota(tile_start[:, :], pattern=[[P, TILES]], base=0, channel_multiplier=0,
                      allow_small_or_imprecise_dtypes=True).then_inc(const_done, 1)
            pool.iota(rank_step[:, :], pattern=[[P, B]], base=0, channel_multiplier=0,
                      allow_small_or_imprecise_dtypes=True).then_inc(const_done, 1)
            pool.iota(prefer_low[:, :], pattern=[[-1, E]], base=E, channel_multiplier=0,
                      allow_small_or_imprecise_dtypes=True).then_inc(const_done, 1)
            pool.iota(token_code[:, :], pattern=[[-P, B]], base=NTOK, channel_multiplier=-1,
                      allow_small_or_imprecise_dtypes=True).then_inc(const_done, 1)
            pool.memset(ones[:, :], 1.0).then_inc(const_done, 1)
            pool.memset(before[:, :], 1.0).then_inc(zeroed, 1)
            pool.memset(e_before[:, :, :], 1.0).then_inc(zeroed, 1)
            pool.wait_ge(zeroed, 6)
            pool.affine_select(before[:, :], before[:, :], pattern=[[1, P]], compare_op=ALU.is_ge, fill=0.0,
                               base=-1, channel_multiplier=-1).then_inc(const_done, 1)
            pool.affine_select(e_before[:, :, :], e_before[:, :, :], pattern=[[1, E], [-1, E]], compare_op=ALU.is_ge,
                               fill=0.0, base=-1, channel_multiplier=0).then_inc(const_done, 1)
            for i in range(GATHER_RING):
                pool.memset(gat[i], 0.0).then_inc(gat_zero, 1)
            pool.wait_ge(gat_zero, GATHER_RING)
            pool.wait_ge(scale_store, 16)
            for i in range(2):
                pool.wait_ge(row_store[i], 16 * (B // 2))
            pool.wait_ge(tok_done, 1)

            def gather(t):
                if t >= GATHER_RING:
                    pool.wait_ge(res_done, t - GATHER_RING + 1)
                slot = t % GATHER_RING
                pool.indirect_dma_start(
                    out=gat[slot], out_offset=None, in_=table[:, :],
                    in_offset=bass.IndirectOffsetOnAxis(ap=tok[:, t:t + 1], axis=0),
                    bounds_check=NTOK - 1, oob_is_err=False).then_inc(gathered[slot], 16)

            def scatter(t):
                pool.wait_ge(res_done, t + 1)
                pool.indirect_dma_start(
                    out=out, out_offset=bass.IndirectOffsetOnAxis(ap=tok[:, t:t + 1], axis=0),
                    in_=res[t % RING][:, :], in_offset=None,
                    bounds_check=NTOK - 1, oob_is_err=False).then_inc(scattered[t % RING], 16)

            for t in range(GATHER_RING):
                gather(t)
            for t in range(TILES):
                scatter(t)
                if t + GATHER_RING < TILES:
                    gather(t + GATHER_RING)
            for i in range(RING):
                pool.wait_ge(scattered[i], 16 * len(range(i, TILES, RING)))

        @block.scalar
        def _(act):
            def zero(n):
                cols = slice(ZERO_SPLIT[n], ZERO_SPLIT[n + 1])
                act.activation(v_flat[:, cols], zero_col[:, :].broadcast_to([P, cols.stop - cols.start]),
                               ACT.Copy).then_inc(vbd_zero, 1)

            def first_values(g):
                js = slice(g * J, g * J + J)
                act.wait_ge(v_mm, g + 1)
                act.wait_ge(vbd_zero, 1 + len(ZERO_SPLIT))
                for odd in range(2):
                    half = slice(odd * HEAD_ROWS, (odd + 1) * HEAD_ROWS)
                    pairs = bank[g][half, :].rearrange("l (j c o d) -> l j c o d", j=J, c=CA, o=2)
                    for chunks, own in OWN:
                        cols = slice(own.start + odd, own.stop + odd, own.step)
                        last = act.activation(v_bd[half, cols, js, 0:HD].rearrange("l c j d -> l j c d"),
                                              pairs[:, :, chunks, odd, :], ACT.Copy)
                last.then_inc(v_done, 1)

            def norms(g):
                act.wait_ge(xt_mm, g + 1)
                if g >= 2:
                    act.wait_ge(q_mm, g - 1)
                act.activation(xn1_t[:, g % 2, :, :].rearrange("p j s -> p (j s)"), XT_BANK[g][:, :],
                               ACT.Copy).then_inc(xt_done, 1)

            def queries(g):
                js = slice(g * J, g * J + J)
                act.wait_ge(q_mm, g + 1)
                act.activation(q_t[:, js, :].rearrange("p j s -> p (j s)"), Q_BANK[g][:, :],
                               ACT.Identity, bias=wrep[:, 2, HD:HV]).then_inc(q_done, 1)

            act.wait_ge(cols_ready, 2)
            zero(0)
            for g in range(G):
                act.wait_ge(ctxt_mm, g + 1)
                keys = bank[g][:, 0:J * L].rearrange("p (j a l) -> p j a l", j=J, a=1)
                act.activation(ctx_t[:, g * J:g * J + J, 0:P].rearrange("p j (a l) -> p j a l", a=2),
                               keys[:, :, :, 0:HEAD_ROWS].broadcast_to([P, J, 2, HEAD_ROWS]), ACT.Copy).then_inc(ctxt_done, 1)
                if g + 1 < G:
                    zero(g + 1)
            act.wait_ge(wrep_done, 1)
            for g in range(G):
                if g == 2:
                    act.wait_ge(rstd1_step, 1)
                    act.activation(guess1[:, :], half_var1[:, :].bitcast(I32), ACT.Exp, scale=GUESS_SCALE,
                                   bias=guess_bias[:, :]).then_inc(guess1_done, 1)
                act.wait_ge(k_mm, g + 1)
                act.activation(k_t[:, g * J:g * J + J, :], bank[4 + g % 2][:, 0:J * L].rearrange("p (j l) -> p j l", j=J),
                               ACT.Identity, bias=wrep[:, 0, HD:HV]).then_inc(k_done, 1)
            act.wait_ge(ld_misc, 64)
            act.activation(tanhs[:, :], gates[:, :], ACT.Tanh).then_inc(tanh_done, 1)
            act.wait_ge(tanh_done, 1)
            act.activation(wo_g[:, :], wo_sb[:, :], ACT.Copy, scale=tanhs[:, 0:1]).then_inc(wog_done, 1)
            first_values(0)
            norms(0)
            first_values(1)
            queries(0)
            norms(1)
            first_values(2)
            queries(1)
            first_values(3)
            norms(2)
            norms(3)
            queries(2)
            queries(3)

            def copy_norms(b):
                act.wait_ge(x2t_mm, b + 1)
                act.activation(xn2_t[:, :], M0[:, 0:P], ACT.Copy).then_inc(x2t_done, 1)

            def copy_attn(b):
                act.wait_ge(at_mm, b + 1)
                act.activation(attn_t[:, :], M0[:, 0:P], ACT.Copy).then_inc(at_done, 1)

            def guess_inverse_std(b):
                act.wait_ge(hv2_done, b + 1)
                act.activation(guess2[:, :], half_var2[:, :].bitcast(I32), ACT.Exp, scale=GUESS_SCALE,
                               bias=guess_bias[:, :]).then_inc(guess2_done, 1)

            def attention(b, k):
                if 2 <= k + 1 < B:
                    round_keys(act, b + 1, k + 1)
                if k >= 1:
                    copy_attn(b - 1)
                for n, (c0, c1) in enumerate(T_CHUNKS):
                    if n == T_BANKS - 1 and k >= 2:
                        copy_norms(b - 2)
                    act.wait_ge(score_mm, b * T_BANKS + n + 1)
                    rows_used = P if c1 <= CA else TAIL_ROWS
                    act.activation(probs[0:rows_used, c0 * P:c1 * P], bank[3 + n][0:rows_used, 0:(c1 - c0) * P], ACT.Exp,
                                   scale=SCALE).then_inc(exp_done, 1)
                if k >= 1:
                    guess_inverse_std(b - 1)

            for_seqs(act, attention)
            copy_attn(B - 1)
            copy_norms(B - 2)
            guess_inverse_std(B - 1)
            copy_norms(B - 1)
            act.wait_ge(lsub_done, 1)
            act.activation(lexp[:, :, :], lsub[:, :, :], ACT.Exp).then_inc(lexp_done, 1)
            act.activation(gelu_warm[:, :], zero_col[:, :], ACT.Gelu_apprx_tanh)
            act.wait_ge(ld_b1, 16)
            act.wait_ge(expert_done, 1)

            def gelu(t, k):
                e = act.value_load(expert[0:1, bass.ds(t, 1)], min_val=0, max_val=E - 1)
                act.wait_ge(up_mm, t + 1)
                for c in range(FC):
                    last = act.activation(hid[:, k % 2, c, :], bank[2 + k % 2][:, c * P:c * P + P], ACT.Gelu_apprx_tanh,
                                          bias=b1_sb[:, bass.ds(e, 1), c])
                last.then_inc(hid_done, 1)

            for_tiles(act, gelu)

        @block.tensor
        def _(pe):
            def stay_busy(n):
                for _ in range(n):
                    pe.matmul(M0[:, :], busy_src[:, 0:P], busy_src[:, :], start=True, stop=True)

            pe.wait_ge(busy_ready, 1)
            stay_busy(6)
            pe.wait_ge(const_done, 2)
            wbd_k, wbd_v, wbd_q = (wbd[:, n, :, :].rearrange("p h d -> p (h d)") for n in range(3))

            def keys(g):
                pe.wait_ge(ctxt_done, g + 1)
                pe.wait_ge(ctxtail_done, g + 1)
                if g >= 2:
                    pe.wait_ge(k_done, g - 1)
                pe.matmul(bank[4 + g % 2][:, 0:J * L], wbd_k, ctx_t[:, g * J:g * J + J, HEAD_ROWS:HEAD_ROWS + L],
                          start=True, stop=True).then_inc(k_mm, 1)

            def values(g):
                for j in range(J):
                    last = pe.matmul(bank[g][:, j * D:j * D + D], ctx_t[:, g * J + j, 0:P], wbd_v,
                                     start=(j == 0), stop=(j == J - 1), skip_group_check=True)
                last.then_inc(v_mm, 1)
                if g < 2:
                    pe.wait_ge(k_done, g + 3)
                else:
                    pe.wait_ge(vtail_done, g - 1)
                for j in range(J):
                    last = pe.matmul(bank[4 + g % 2][0:TAIL_ROWS, j * D:j * D + D], ctx_t[:, g * J + j, P:P + TAIL_ROWS],
                                     wbd_v, start=(j == 0), stop=(j == J - 1), skip_group_check=True)
                last.then_inc(vtail_mm, 1)

            def norms(g):
                pe.wait_ge(xn1_done, (g + 1) * J)
                if g == 1:
                    pe.wait_ge(xt_done, 1)
                if g >= 2:
                    pe.wait_ge(vtail_done, g + 1)
                for j in range(J):
                    last = pe.transpose(XT_BANK[g][:, j * P:j * P + P], xn1[:, g * J + j, :], ident[:, :])
                last.then_inc(xt_mm, 1)

            def queries(g):
                pe.wait_ge(xt_done, g + 1)
                if g == 0:
                    pe.wait_ge(obias_done, 1)
                elif g < 3:
                    pe.wait_ge(q_done, g)
                pe.matmul(Q_BANK[g][:, :], wbd_q, xn1_t[:, g % 2, :, :].rearrange("p j s -> p (j s)"),
                          start=True, stop=True).then_inc(q_mm, 1)

            for g in range(G):
                pe.wait_ge(ld_ctx[g], 16)
                for j in range(J):
                    last = pe.transpose(bank[g][:, j * L:j * L + L], ctx_sb[:, g * J + j, :], ident[0:L, 0:L])
                last.then_inc(ctxt_mm, 1)
                if g == 0:
                    pe.wait_ge(ld_small, 16)
                    pe.matmul(bank[7][:, 0:3 * HV], rep[:, :], w_small[:, :, :].rearrange("p n d -> p (n d)"),
                              start=True, stop=True).then_inc(wrep_mm, 1)
                    pe.wait_ge(wbd_done, 1)
                else:
                    keys(g - 1)
                if g + 1 < G:
                    stay_busy(1)
            keys(G - 1)
            values(0)
            pe.wait_ge(bvc_done, 1)
            pe.wait_ge(wog_done, 1)
            pe.matmul(bank[7][:, 0:D], bv_cols[:, :], wo_g[:, :], start=True, stop=True).then_inc(obias_mm, 1)
            norms(0)
            values(1)
            queries(0)
            norms(1)
            values(2)
            queries(1)
            values(3)
            norms(2)
            norms(3)
            queries(2)
            queries(3)

            def energies(b, k):
                if k < 2:
                    pe.wait_ge(keysb_first, k + 1)
                else:
                    pe.wait_ge(keysb_ready, b - 1)
                for n, (h0, h1) in enumerate(E_HEADS):
                    last = pe.matmul(bank[n][:, 0:(h1 - h0) * L],
                                     q_tb[:, bass.ds(b, 1), :].rearrange("p a s -> p (a s)"),
                                     k_bdb[:, k % 2, h0 * L:h1 * L], start=True, stop=True)
                last.then_inc(energy_mm, 1)

            def scores(b, k, n):
                c0, c1 = T_CHUNKS[n]
                for c in range(c0, c1):
                    m, at = chunk_rows(c)
                    pe.matmul(bank[3 + n][0:m, (c - c0) * P:(c - c0) * P + P], k_bd[:, k % 2, at:at + m],
                              q_t[:, bass.ds(b, 1), :].rearrange("p a s -> p (a s)"), start=(c == c0), stop=False,
                              skip_group_check=True)

            def shift_scores(n):
                c0, c1 = T_CHUNKS[n]
                for c in range(c0, c1):
                    m, at = chunk_rows(c)
                    last = pe.matmul(bank[3 + n][0:m, (c - c0) * P:(c - c0) * P + P], headsel[:, at:at + m],
                                     shift_t[:, :], start=False, stop=(c == c1 - 1), skip_group_check=True)
                last.then_inc(score_mm, 1)

            def attn_transpose(b, k):
                pe.wait_ge(attn_done, b + 1)
                if k >= 2:
                    pe.wait_ge(lg_done, b - 1)
                pe.transpose(M0[:, 0:P], attn[:, :], ident[:, :]).then_inc(at_mm, 1)

            def project_out(b):
                pe.wait_ge(at_done, b + 1)
                pe.matmul(M0[:, 0:D], attn_t[:, :], wo_g[:, :], start=True, stop=True).then_inc(wo_mm, 1)

            def norm_transpose(b, k):
                pe.wait_ge(xn2_done, b + 1)
                pe.transpose(M0[:, 0:P], rows[:, k % 2, D:2 * D], ident[:, :]).then_inc(x2t_mm, 1)

            def router(b):
                pe.wait_ge(x2t_done, b + 1)
                pe.matmul(M0[:, 0:E], xn2_t[:, :], sw_sb[:, :], start=True, stop=True).then_inc(lg_mm, 1)

            def weigh_values(b, n):
                pe.wait_ge(exp_done, b * T_BANKS + n + 1)
                for c in range(*T_CHUNKS[n]):
                    m, _ = chunk_rows(c)
                    last = pe.matmul(M1[:, W0[c] * HV:(W0[c] + W) * HV], probs[0:m, c * P:c * P + P],
                                     v_bd[0:m, c * W:(c + 1) * W, bass.ds(b, 1), :].rearrange("p h b d -> p h (b d)"),
                                     start=(c == 0), stop=(c == CH - 1), skip_group_check=True)
                if n == T_BANKS - 1:
                    last.then_inc(pv_mm, 1)

            def attention(b, k):
                scores(b, k, 0)
                if k == 0:
                    pe.wait_ge(q_done, 3)
                    pe.wait_ge(sel_done, 3)
                    pe.wait_ge(identb_done, 1)
                if k == 1:
                    pe.wait_ge(q_done, G)
                    pe.wait_ge(qb_done, G)
                    pe.wait_ge(ld_router, 32)
                if k >= 1:
                    attn_transpose(b - 1, k - 1)
                pe.wait_ge(shift_done, b + 1)
                pe.transpose(M1.bitcast(BF16)[:, 0:P], shift[:, k % 2, :], identb[:, :]).then_inc(shiftt_mm, 1)
                scores(b, k, 1)
                pe.wait_ge(shiftt_done, b + 1)
                shift_scores(0)
                shift_scores(1)
                if k >= 1:
                    project_out(b - 1)
                scores(b, k, 2)
                shift_scores(2)
                if k + 1 < B:
                    energies(b + 1, k + 1)
                if k >= 2:
                    pe.wait_ge(x1_done, b)
                    norm_transpose(b - 2, k - 2)
                if k == 0:
                    pe.wait_ge(v_ones, 6)
                weigh_values(b, 0)
                if k >= 2:
                    router(b - 2)
                weigh_values(b, 1)
                weigh_values(b, 2)

            pe.wait_ge(v_done, G)
            pe.wait_ge(qb_done, 1)
            energies(0, 0)
            for_seqs(pe, attention)
            attn_transpose(B - 1, B - 1)
            project_out(B - 1)
            pe.wait_ge(x1_done, B)
            norm_transpose(B - 2, B - 2)
            router(B - 2)
            pe.wait_ge(lg_done, B - 1)
            norm_transpose(B - 1, B - 1)
            router(B - 1)

            pe.wait_ge(oh_done, 1)
            pe.wait_ge(const_done, 13)
            pe.matmul(bank[0][:, 0:B * E], before[:, :], onehotb[:, :, :].rearrange("p b e -> p (b e)"),
                      start=True, stop=False, skip_group_check=True)
            for b in range(B):
                last = pe.matmul(bank[0][:, (b + 1) * E:(B + 1) * E].rearrange("p (n e) -> p n e", e=E), ones[:, :],
                                 onehotb[:, b:b + 1, :].broadcast_to([P, B - b, E]),
                                 start=False, stop=(b == B - 1), skip_group_check=True)
            last.then_inc(rank_mm, 1)
            pe.wait_ge(tilecode_done, 1)
            for b in range(B):
                pe.wait_ge(rowhot_done, b + 1)
                last = pe.matmul(bank[1][:, 0:TILES], row_hot[:, b, :], tile_code[:, b, :], start=(b == 0), stop=(b == B - 1))
            last.then_inc(tok_mm, 1)
            stay_busy(8)
            pe.wait_ge(ld_w2, 16)
            pe.wait_ge(expert_done, 1)

            def rows_transpose(t, k):
                slot = k % GATHER_RING
                pe.wait_ge(gathered[slot], fill_count(t, k, GATHER_RING))
                pe.transpose(bank[k % 2][:, 0:P], gat[slot][:, D:2 * D], ident[:, :]).then_inc(xgt_mm, 1)

            def up(t, k):
                pe.wait_ge(xgt_done, t + 1)
                pe.wait_ge(w1_ready[k % RING], fill_count(t, k, RING))
                for c in range(FC):
                    last = pe.matmul(bank[2 + k % 2][:, c * P:c * P + P], w1_ring[:, k % RING, c * P:c * P + P],
                                     xg_t[:, k % 2, :], start=(c == 0), stop=(c == FC - 1), skip_group_check=True)
                last.then_inc(up_mm, 1)

            def down(t, k):
                e = pe.value_load(expert[0:1, bass.ds(t, 1)], min_val=0, max_val=E - 1)
                pe.wait_ge(hid_done, t + 1)
                if k >= 2:
                    pe.wait_ge(yb_done, t - 1)
                for c in range(FC):
                    last = pe.matmul(bank[4 + k % 2][:, 0:D], hid[:, k % 2, c, :],
                                     w2_sb[:, bass.ds(e, 1), c, :].rearrange("p a d -> p (a d)"),
                                     start=(c == 0), stop=(c == FC - 1))
                last.then_inc(down_mm, 1)

            def ffn(t, k):
                if k == 1:
                    up(0, 0)
                rows_transpose(t, k)
                if k >= 2:
                    up(t - 1, k - 1)
                    down(t - 2, k - 2)

            for_tiles(pe, ffn)
            up(TILES - 1, TILES - 1)
            down(TILES - 2, TILES - 2)
            down(TILES - 1, TILES - 1)

        @block.vector
        def _(dve):
            dve.memset(busy_src[:, :], 0.0).then_inc(busy_ready, 1)
            dve.memset(v_flat[:, 0:ZERO_SPLIT[0]], 0.0).then_inc(vbd_zero, 1)
            dve.wait_ge(wrep_mm, 1)
            dve.tensor_copy(wrep[:, :, :], bank[7][:, 0:3 * HV].rearrange("p (n d) -> p n d", n=3)).then_inc(wrep_done, 1)
            dve.wait_ge(wrep_done, 1)
            dve.wait_ge(const_done, 3)
            for n in range(3):
                last = dve.tensor_tensor(wbd[:, n, :, :], wrep[:, n:n + 1, 0:HD].broadcast_to([P, H, HD]),
                                         headmask[:, :].rearrange("p (h a) -> p h a", a=1).broadcast_to([P, H, HD]),
                                         ALU.mult)
            last.then_inc(wbd_done, 1)
            dve.tensor_copy(bv_cols[:, :], wrep[:, 1, HD:HV].broadcast_to([P, P])).then_inc(bvc_done, 1)
            for g in range(G):
                dve.wait_ge(ctxt_done, g + 1)
                keys = bank[g][:, 0:J * L].rearrange("p (j a l) -> p j a l", j=J, a=1)
                dve.tensor_copy(ctx_t[:, g * J:g * J + J, P:P + TAIL_ROWS].rearrange("p j (a l) -> p j a l", a=TAIL_HEADS),
                                keys[:, :, :, HEAD_ROWS:L].broadcast_to([P, J, TAIL_HEADS, TAIL_KEYS])).then_inc(ctxtail_done, 1)
                dve.wait_ge(ld_x[g], 16)
                for b in range(g * J, g * J + J):
                    dve.bn_stats(stats1[:, b, :], x_sb[:, b, :]).then_inc(st1_done, 1)
                for b in range(g * J, g * J + J):
                    dve.wait_ge(st1_done, b + 1)
                    dve.bn_aggr(mv1[:, b, :], stats1[:, b, :]).then_inc(mv1_done, 1)
            dve.wait_ge(mv1_done, B)
            dve.tensor_scalar(half_var1[:, :], mv1[:, :, 1], EPS, 0.5, ALU.add, ALU.mult).then_inc(rstd1_step, 1)
            dve.wait_ge(rstd1_step, 1)
            dve.wait_ge(guess1_done, 1)
            for n, (y, better) in enumerate(((guess1, rstd1), (rstd1, rstd1))):
                dve.tensor_tensor(newton1[:, :], y[:, :], half_var1[:, :], ALU.mult).then_inc(rstd1_step, 1)
                dve.wait_ge(rstd1_step, 3 * n + 2)
                dve.tensor_tensor(newton1[:, :], newton1[:, :], y[:, :], ALU.mult).then_inc(rstd1_step, 1)
                dve.wait_ge(rstd1_step, 3 * n + 3)
                dve.scalar_tensor_tensor(better[:, :], newton1[:, :], 1.5, y[:, :], ALU.subtract, ALU.mult,
                                         reverse0=True).then_inc(rstd1_step, 1)
                dve.wait_ge(rstd1_step, 3 * n + 4)

            def norms(g):
                for b in range(g * J, g * J + J):
                    dve.tensor_scalar(xn1[:, b, :], x_sb[:, b, :], mv1[:, b, 0:1], rstd1[:, b:b + 1],
                                      ALU.subtract, ALU.mult).then_inc(xn1_done, 1)

            def other_values(g):
                js = slice(g * J, g * J + J)
                dve.wait_ge(vtail_mm, g + 1)
                for n in range(2):
                    h0 = (CA + n) * W + n * TAIL_HEADS - W0[CA + n]
                    last = dve.tensor_tensor(
                        v_bd[0:TAIL_ROWS, h0:h0 + TAIL_HEADS, js, 0:HD].rearrange("l h j d -> l j h d"),
                        bank[4 + g % 2][0:TAIL_ROWS, :].rearrange("l (j n h d) -> l j n h d", j=J, n=2, d=HD)[:, :, n, :, :],
                        tailmask[0:TAIL_ROWS, :].rearrange("p (a h b) -> p a h b", a=1, b=1)
                        .broadcast_to([TAIL_ROWS, J, TAIL_HEADS, HD]), ALU.mult)
                last.then_inc(vtail_done, 1)

            norms(0)
            norms(1)
            dve.wait_ge(obias_mm, 1)
            dve.scalar_tensor_tensor(out_bias[:, :], bo_bc[:, :], tanhs[:, 0:1], bank[7][:, 0:D],
                                     ALU.mult, ALU.add).then_inc(obias_done, 1)
            dve.wait_ge(vbd_zero, 1 + len(ZERO_SPLIT))
            dve.wait_ge(const_done, 4)
            other_values(0)
            norms(2)
            other_values(1)
            norms(3)
            other_values(2)
            dve.tensor_tensor(sel[:, :], ident[:, 0:H], ident[:, H:2 * H], ALU.add).then_inc(sel_done, 1)
            dve.wait_ge(sel_done, 1)
            at = 0
            for keys in (HEAD_ROWS, TAIL_KEYS):
                dve.tensor_copy(headsel[:, at:at + H * keys].rearrange("p (h l) -> p h l", h=H),
                                sel[:, :].rearrange("p (h a) -> p h a", a=1).broadcast_to([P, H, keys])
                                ).then_inc(sel_done, 1)
                at += H * keys
            dve.tensor_copy(identb[:, :], ident[:, :]).then_inc(identb_done, 1)

            def round_first_keys(b):
                dve.wait_ge(keys_ready, b + 1)
                for part, keys in KEY_PARTS:
                    last = dve.tensor_copy(k_bdb[:, b, :].rearrange("p (h l) -> p h l", h=H)[:, :, keys],
                                           k_bd[:, b, part].rearrange("p (h l) -> p h l", h=H))
                last.then_inc(keysb_first, 1)

            def round_queries(g):
                js = slice(g * J, g * J + J)
                dve.wait_ge(q_done, g + 1)
                dve.tensor_copy(q_tb[:, js, :], q_t[:, js, :]).then_inc(qb_done, 1)

            round_first_keys(0)
            other_values(3)
            round_queries(0)
            round_first_keys(1)

            def row_max(b, k):
                dve.wait_ge(energy_mm, b + 1)
                full = [n for n, (h0, h1) in enumerate(E_HEADS) if h1 - h0 == PER_BANK]
                dve.tensor_reduce(emax[:, k % 2, 0:len(full) * PER_BANK].rearrange("p (n h) -> p n h", n=len(full)),
                                  ps_e[:, 0:len(full), 0:PER_BANK * L].rearrange("p n (h l) -> p n h l", l=L),
                                  AX, ALU.max)
                h0, h1 = E_HEADS[-1]
                dve.tensor_reduce(emax[:, k % 2, h0:h1], ps_e[:, E_BANKS - 1, 0:(h1 - h0) * L]
                                  .rearrange("p (h l) -> p h l", l=L), AX, ALU.max).then_inc(emax_done, 1)

            def split_shift(b, k):
                dve.wait_ge(emax_done, b + 1)
                dve.tensor_scalar(shift[:, k % 2, 0:H], emax[:, k % 2, :], -1.0, None, ALU.mult).then_inc(shift1_done, 1)
                dve.wait_ge(shift1_done, b + 1)
                dve.scalar_tensor_tensor(shift[:, k % 2, H:2 * H], emax[:, k % 2, :], -1.0, shift[:, k % 2, 0:H],
                                         ALU.mult, ALU.subtract).then_inc(shift_done, 1)

            def normalise(b):
                dve.wait_ge(pv_mm, b + 1)
                o = M1[:, 0:H * HV].rearrange("p (h d) -> p h d", h=H)
                dve.reciprocal(rden[:, :], o[:, :, HD]).then_inc(rden_done, 1)
                dve.wait_ge(rden_done, b + 1)
                dve.tensor_tensor(attn[:, :].rearrange("p (h d) -> p h d", h=H), o[:, :, 0:HD],
                                  rden[:, :].rearrange("p (h a) -> p h a", a=1).broadcast_to([P, H, HD]),
                                  ALU.mult).then_inc(attn_done, 1)

            def residual_norm(b, k, row_wait):
                dve.wait_ge(wo_mm, b + 1)
                if k == 0:
                    dve.wait_ge(xres_done, 1)
                if k == 2:
                    dve.wait_ge(xres_done, G)
                if row_wait is not None:
                    dve.wait_ge(row_store[k % 2], row_wait)
                x1 = rows[:, k % 2, 0:D]
                dve.tensor_tensor(x1, M0[:, 0:D], x_sb[:, bass.ds(b, 1), :].rearrange("p a d -> p (a d)"),
                                  ALU.add).then_inc(x1_done, 1)
                dve.wait_ge(x1_done, b + 1)
                dve.bn_stats(stats2[:, :], x1).then_inc(st2_done, 1)
                dve.wait_ge(st2_done, b + 1)
                detach(dve)
                dve.bn_aggr(mv2[:, :], stats2[:, :]).then_inc(mv2_done, 1)
                dve.wait_ge(mv2_done, b + 1)
                dve.tensor_scalar(half_var2[:, :], mv2[:, 1:2], EPS, 0.5, ALU.add, ALU.mult).then_inc(hv2_done, 1)

            def newton_step(b, n):
                if n == 0:
                    dve.wait_ge(guess2_done, b + 1)
                else:
                    dve.wait_ge(rstd2_step, b * 4 + 2)
                y = (guess2, rstd2)[n]
                dve.tensor_scalar(newton2[:, :], y[:, :], y[:, :], half_var2[:, :],
                                  ALU.mult, ALU.mult).then_inc(rstd2_step, 1)
                dve.wait_ge(rstd2_step, b * 4 + (2 * n + 1))
                dve.scalar_tensor_tensor(rstd2[:, :], newton2[:, :], 1.5, y[:, :], ALU.subtract, ALU.mult,
                                         reverse0=True).then_inc(rstd2_step, 1)

            def norm(b, k):
                dve.wait_ge(rstd2_step, b * 4 + 4)
                dve.tensor_scalar(rows[:, k % 2, D:2 * D], rows[:, k % 2, 0:D], mv2[:, 0:1], rstd2[:, 0:1],
                                  ALU.subtract, ALU.mult).then_inc(xn2_done, 1)

            def router_bias(b):
                dve.wait_ge(lg_mm, b + 1)
                dve.tensor_tensor(logits[:, bass.ds(b, 1), :].rearrange("p a e -> p (a e)"), M0[:, 0:E], sbias[:, :],
                                  ALU.add).then_inc(lg_done, 1)

            def copy_shift(b, k):
                dve.wait_ge(shiftt_mm, b + 1)
                dve.tensor_copy(shift_t[:, :], M1.bitcast(BF16)[:, 0:P]).then_inc(shiftt_done, 1)

            def attention(b, k):
                if k >= 1:
                    normalise(b - 1)
                if k >= 2:
                    newton_step(b - 2, 0)
                    copy_shift(b, k)
                    newton_step(b - 2, 1)
                    norm(b - 2, k - 2)
                if k < 2:
                    copy_shift(b, k)
                if k == 0:
                    for g in range(1, G):
                        round_queries(g)
                if k >= 1:
                    stores = (b - 1 - (k - 1) % 2) * 8 if k >= 3 else None
                    residual_norm(b - 1, k - 1, stores)
                if k + 1 < B:
                    row_max(b + 1, k + 1)
                if k >= 2:
                    router_bias(b - 2)
                if k + 1 < B:
                    split_shift(b + 1, k + 1)

            dve.wait_ge(pad_zero, 1)
            dve.wait_ge(ld_router, 32)
            row_max(0, 0)
            split_shift(0, 0)
            for_seqs(dve, attention)
            normalise(B - 1)
            newton_step(B - 2, 0)
            newton_step(B - 2, 1)
            norm(B - 2, B - 2)
            residual_norm(B - 1, B - 1, (B - 1 - (B - 1) % 2) * 8)
            router_bias(B - 2)
            newton_step(B - 1, 0)
            newton_step(B - 1, 1)
            norm(B - 1, B - 1)
            router_bias(B - 1)

            done = [0]

            def step(ins):
                ins.then_inc(route_step, 1)
                done[0] += 1
                dve.wait_ge(route_step, done[0])

            def over_e(ap):
                return ap.rearrange("p (b a) -> p b a", a=1).broadcast_to([P, B, E])

            dve.wait_ge(lg_done, B)
            dve.wait_ge(const_done, 13)
            step(dve.tensor_reduce(lmax[:, :], logits[:, :, :], AX, ALU.max))
            dve.tensor_tensor(lsub[:, :, :], logits[:, :, :], over_e(lmax[:, :]), ALU.subtract).then_inc(lsub_done, 1)
            dve.wait_ge(lsub_done, 1)
            step(dve.scalar_tensor_tensor(is_max[:, :, :], lsub[:, :, :], 0.0,
                                          prefer_low[:, :].rearrange("p (a e) -> p a e", a=1).broadcast_to([P, B, E]),
                                          ALU.is_equal, ALU.mult))
            step(dve.tensor_reduce(pick[:, :], is_max[:, :, :], AX, ALU.max))
            dve.tensor_tensor(onehotb[:, :, :], is_max[:, :, :], over_e(pick[:, :]), ALU.is_equal).then_inc(oh_done, 1)
            dve.wait_ge(lexp_done, 1)
            step(dve.tensor_reduce(lsum[:, :], lexp[:, :, :], AX, ALU.add))
            step(dve.reciprocal(lsum[:, :], lsum[:, :]))
            dve.tensor_scalar(scale_tok[:, :], lsum[:, :], tanhs[:, 1:2], None, ALU.mult).then_inc(scale_done, 1)
            dve.wait_ge(rank_mm, 1)
            count = bank[0][:, B * E:(B + 1) * E]
            step(dve.tensor_tensor(over[:, :, :], count.rearrange("p (e a) -> p e a", a=1).broadcast_to([P, E, B]),
                                   rank_step[:, :].rearrange("p (a b) -> p a b", a=1).broadcast_to([P, E, B]),
                                   ALU.is_gt))
            step(dve.tensor_reduce(n_tiles[:, :], over[:, :, :], AX, ALU.add))
            step(dve.tensor_tensor(base_prod[:, :, :], e_before[:, :, :],
                                   n_tiles[:, :].rearrange("p (a e) -> p a e", a=1).broadcast_to([P, E, E]), ALU.mult))
            dve.tensor_reduce(base[:, :], base_prod[:, :, :], AX, ALU.add).then_inc(base_done, 1)
            dve.wait_ge(base_done, 1)
            dve.tensor_tensor(end[:, :], base[0:1, :], n_tiles[0:1, :], ALU.add).then_inc(expert_step, 1)
            step(dve.scalar_tensor_tensor(slot_e[:, :, :], base[:, :].rearrange("p (a e) -> p a e", a=1).broadcast_to([P, B, E]),
                                          float(P), bank[0][:, 0:B * E].rearrange("p (b e) -> p b e", e=E),
                                          ALU.mult, ALU.add))
            dve.wait_ge(expert_step, 1)
            step(dve.tensor_tensor(slot_m[:, :, :], slot_e[:, :, :], onehotb[:, :, :], ALU.mult))
            dve.tensor_tensor(past[:, :, :], tile_no[:, :].rearrange("p (t a) -> p t a", a=1).broadcast_to([1, TILES, E]),
                              end[:, :].rearrange("p (a e) -> p a e", a=1).broadcast_to([1, TILES, E]),
                              ALU.is_ge).then_inc(expert_step, 1)
            step(dve.tensor_reduce(slot[:, :], slot_m[:, :, :], AX, ALU.add))
            dve.wait_ge(expert_step, 2)
            dve.tensor_reduce(expert_f[:, :], past[:, :, :], AX, ALU.add).then_inc(expert_step, 1)
            step(dve.tensor_copy(slot_int[:, :], slot[:, :]))
            dve.wait_ge(expert_step, 3)
            dve.tensor_scalar(expert[:, :], expert_f[:, :], float(E - 1), None, ALU.min).then_inc(expert_done, 1)
            step(dve.tensor_scalar(slot_low[:, :], slot_int[:, :], P - 1, None, ALU.bitwise_and))
            dve.tensor_copy(slot_row[:, :], slot_low[:, :]).then_inc(slotrow_done, 1)
            dve.wait_ge(slotrow_done, 1)
            step(dve.tensor_tensor(slot_start[:, :], slot[:, :], slot_row[:, :], ALU.subtract))
            dve.tensor_tensor(tile_hot[:, :, :],
                              tile_start[:, :].rearrange("p (a t) -> p a t", a=1).broadcast_to([P, B, TILES]),
                              slot_start[:, :].rearrange("p (b a) -> p b a", a=1).broadcast_to([P, B, TILES]),
                              ALU.is_equal).then_inc(tilehot_done, 1)
            dve.wait_ge(tilehot_done, 1)
            dve.tensor_tensor(tile_code[:, :, :], tile_hot[:, :, :],
                              token_code[:, :].rearrange("p (b a) -> p b a", a=1).broadcast_to([P, B, TILES]),
                              ALU.mult).then_inc(tilecode_done, 1)
            for b in range(B):
                dve.tensor_scalar(row_hot[:, b, :], iota_row[:, :], slot_row[:, b:b + 1], None,
                                  ALU.is_equal).then_inc(rowhot_done, 1)
            dve.wait_ge(tok_mm, 1)
            dve.tensor_scalar(tok[:, :], bank[1][:, 0:TILES], -1.0, float(NTOK), ALU.mult, ALU.add).then_inc(tok_done, 1)
            dve.wait_ge(ld_b2, 16)

            def rows_copy(t, k):
                dve.wait_ge(xgt_mm, t + 1)
                dve.tensor_copy(xg_t[:, k % 2, :], bank[k % 2][:, 0:P]).then_inc(xgt_done, 1)

            def combine(t, k, scatter_wait):
                e = dve.value_load(expert[0:1, bass.ds(t, 1)], min_val=0, max_val=E - 1)
                dve.wait_ge(down_mm, t + 1)
                dve.tensor_tensor(yb[:, k % 2, :], bank[4 + k % 2][:, 0:D],
                                  b2_bc[:, bass.ds(e, 1), :].rearrange("p a d -> p (a d)"), ALU.add).then_inc(yb_done, 1)
                dve.wait_ge(yb_done, t + 1)
                if scatter_wait is not None:
                    dve.wait_ge(scattered[k % RING], scatter_wait)
                g = gat[k % GATHER_RING]
                dve.scalar_tensor_tensor(res[k % RING][:, :], yb[:, k % 2, :], g[:, 2 * D:ROW], g[:, 0:D],
                                         ALU.mult, ALU.add).then_inc(res_done, 1)

            def scatters_before(t, k):
                return (t - k % RING) * (16 // RING) if k >= RING else None

            def rows_and_results(t, k):
                rows_copy(t, k)
                if k >= 2:
                    combine(t - 2, k - 2, scatters_before(t - 2, k - 2))

            for_tiles(dve, rows_and_results)
            for t in range(TILES - 2, TILES):
                combine(t, t, scatters_before(t, t))


_HEAD_WEIGHTS = [("L0_xattn_wk", "L0_xattn_bk"), ("L0_xattn_wv", "L0_xattn_bv"), ("L0_xattn_wq", "L0_xattn_bq")]
_AS_THEY_ARE = ["L0_xattn_bo", "L0_ffn_switch_w", "L0_ffn_switch_b", "L0_ffn_w1"]


def kernel(**inputs):
    import numpy as np
    import concourse.bacc as bacc
    from concourse.bass_utils import run_bass_kernel_spmd

    given = {name: np.asarray(a) for name, a in inputs.items()}
    laid = {name: given[name] for name in ("x", "ctx_1024", "g_xattn", "g_ffn")}
    laid["w_heads"] = np.stack([np.concatenate([given[w].T, given[b][:, None]], axis=1) for w, b in _HEAD_WEIGHTS], axis=1)
    laid["wo_t"] = given["L0_xattn_wo"].T
    laid |= {name: given[name] for name in _AS_THEY_ARE}
    laid["b1_t"] = given["L0_ffn_b1"].reshape(-1, P).T
    laid |= {name: given[name] for name in ("L0_ffn_w2", "L0_ffn_b2")}

    nc = bacc.Bacc("TRN2", target_bir_lowering=False, num_devices=1)
    arrays, args = {}, []
    for name, a in laid.items():
        arrays[f"in_{name}"] = np.ascontiguousarray(a)
        args.append(nc.dram_tensor(f"in_{name}", a.shape, mybir.dt.from_np(a.dtype), kind="ExternalInput").ap())
    B, S, D = inputs["x"].shape
    out = nc.dram_tensor("out_rows", (B * S, D), F32, kind="ExternalOutput").ap()
    table = nc.dram_tensor("row_table", (B * S, 2 * D + 1), F32).ap()
    flamingo_layer(nc, *args, out, table)
    r = run_bass_kernel_spmd(nc, [arrays], core_ids=[0])
    return r.results[0]["out_rows"].reshape(B, S, D)
```
